# Optimizing a Trainium2 kernel written in Bass

```python
import numpy as np
import jax
import jax.numpy as jnp

def _softmax(x, axis=-1):
    return jax.nn.softmax(x, axis=axis)

def _gelu(x):
    return jax.nn.gelu(x, approximate=True)

def _silu(x):
    return jax.nn.silu(x)

def _sigmoid(x):
    return jax.nn.sigmoid(x)

def _layernorm(x, axis=-1, eps=1e-05):
    m = jnp.mean(x, axis=axis, keepdims=True)
    v = jnp.var(x, axis=axis, keepdims=True)
    return (x - m) / jnp.sqrt(v + eps)

def _scatter_add(tgt, idx, src, axis=0):
    return tgt.at[idx].add(src)

def _segment_sum(src, seg, n):
    return jax.ops.segment_sum(src, seg, n)
kernel_name = 'mk_gnn_preln_d2_gnn_r8_a1152a'

def setup_inputs(seed: int=0):
    np.random.seed(seed)
    _w = jnp.asarray

    def _rec_inputs():
        import jax
        import jax.numpy as jnp
        _gk = jax.random.key(seed)
        x = -0.000202 + 1 * jax.random.normal(jax.random.fold_in(_gk, 1), (12500, 64), jnp.float32)
        src = jax.random.randint(jax.random.fold_in(_gk, 2), (400000,), 0, 12500, jnp.int32)
        dst = jax.random.randint(jax.random.fold_in(_gk, 3), (400000,), 0, 12500, jnp.int32)
        _o = jnp.argsort(dst, stable=True)
        src = src[_o]
        dst = dst[_o]
        edge_attr_32 = 0.000164634 + 1.0002 * jax.random.normal(jax.random.fold_in(_gk, 12), (400000, 32), jnp.float32)
        edge_weight = jax.random.uniform(jax.random.fold_in(_gk, 14), (400000,), jnp.float32, 0.0, 1)
        return (x, src, dst, edge_attr_32, edge_weight)
    x, src, dst, edge_attr_32, edge_weight = _rec_inputs()

    def _L0_gnn_setup():
        import jax, jax.numpy as jnp
        import numpy as np
        N_NODES = 12500
        N_EDGES = 200000
        IN_DIM = 64
        OUT_DIM = 64
        key = jax.random.key(seed)
        k1, k2, k3, k4, k5, k6 = jax.random.split(key, 6)
        features = jax.random.normal(k1, (N_NODES, IN_DIM), dtype=jnp.float32)
        src = jax.random.randint(k2, (N_EDGES,), 0, N_NODES, dtype=jnp.int64)
        dst = jax.random.randint(k3, (N_EDGES,), 0, N_NODES, dtype=jnp.int64)
        edge_w = jax.random.uniform(k4, (N_EDGES,), dtype=jnp.float32)
        weight = jax.random.normal(k5, (OUT_DIM, IN_DIM), dtype=jnp.float32) * (1.0 / np.sqrt(IN_DIM))
        b = jax.random.normal(k6, (OUT_DIM,), dtype=jnp.float32) * 0.01
        return {'features': features, 'src': src, 'dst': dst, 'edge_w': edge_w, 'weight': weight, 'b': b}
    _L0_gnn_all = _L0_gnn_setup()
    _L0_gnn_in = {k: v for k, v in _L0_gnn_all.items() if k in ('weight', 'b')}
    del _L0_gnn_all

    def _L1_gnn_setup():
        import jax, jax.numpy as jnp
        import numpy as np
        EPS = 0.0
        key = jax.random.key(seed)
        ks = jax.random.split(key, 8)
        N, E, IN_D, OUT_D, E_D = (6250, 156250, 64, 64, 32)
        x = jax.random.normal(ks[0], (N, IN_D), dtype=jnp.float32)
        edge_index = jax.random.randint(ks[1], (2, E), 0, N, dtype=jnp.int32)
        edge_attr = jax.random.normal(ks[2], (E, E_D), dtype=jnp.float32)
        s = 1.0 / np.sqrt(E_D)
        We = jax.random.uniform(ks[3], (E_D, IN_D), jnp.float32, -s, s)
        be = jnp.zeros((IN_D,), jnp.float32)
        s1 = 1.0 / np.sqrt(IN_D)
        W1 = jax.random.uniform(ks[4], (IN_D, OUT_D), jnp.float32, -s1, s1)
        b1 = jnp.zeros((OUT_D,), jnp.float32)
        s2 = 1.0 / np.sqrt(OUT_D)
        W2 = jax.random.uniform(ks[5], (OUT_D, OUT_D), jnp.float32, -s2, s2)
        b2 = jnp.zeros((OUT_D,), jnp.float32)
        return {'x': x, 'edge_index': edge_index, 'edge_attr': edge_attr, 'We': We, 'be': be, 'W1': W1, 'b1': b1, 'W2': W2, 'b2': b2}
    _L1_gnn_all = _L1_gnn_setup()
    _L1_gnn_in = {k: v for k, v in _L1_gnn_all.items() if k in ('We', 'be', 'W1', 'b1', 'W2', 'b2')}
    del _L1_gnn_all
    return {'x': x, 'src': src, 'dst': dst, 'edge_attr_32': edge_attr_32, 'edge_weight': edge_weight, 'L0_gnn_weight': _L0_gnn_in['weight'], 'L0_gnn_b': _L0_gnn_in['b'], 'L1_gnn_We': _L1_gnn_in['We'], 'L1_gnn_be': _L1_gnn_in['be'], 'L1_gnn_W1': _L1_gnn_in['W1'], 'L1_gnn_b1': _L1_gnn_in['b1'], 'L1_gnn_W2': _L1_gnn_in['W2'], 'L1_gnn_b2': _L1_gnn_in['b2']}

def reference(x, src, dst, edge_attr_32, edge_weight, L0_gnn_weight, L0_gnn_b, L1_gnn_We, L1_gnn_be, L1_gnn_W1, L1_gnn_b1, L1_gnn_W2, L1_gnn_b2):
    import jax
    import jax.numpy as jnp

    def _L0_gnn_ref(features, src, dst, edge_w, weight, b):
        import jax, jax.numpy as jnp
        import numpy as np
        N_NODES = 12500
        N_EDGES = 200000
        IN_DIM = 64
        OUT_DIM = 64
        degs = jax.ops.segment_sum(jnp.ones_like(edge_w), dst, num_segments=N_NODES)
        norm = jnp.where(degs > 0, jax.lax.rsqrt(degs), 0.0)[:, None]
        h = features * norm
        msg = h[src] * edge_w[:, None]
        agg = jax.ops.segment_sum(msg, dst, num_segments=N_NODES)
        h = agg * norm
        return h @ weight.T + b

    def _L1_gnn_ref(x, edge_index, edge_attr, We, be, W1, b1, W2, b2):
        import jax, jax.numpy as jnp
        import numpy as np
        EPS = 0.0
        src, dst = (edge_index[0], edge_index[1])
        msg = jax.nn.relu(x[src] + edge_attr @ We + be)
        aggr = jax.ops.segment_sum(msg, dst, num_segments=x.shape[0])
        h = (1.0 + EPS) * x + aggr
        return jax.nn.relu(h @ W1 + b1) @ W2 + b2
    edge_index = jnp.stack([src, dst])
    h = jnp.maximum(_layernorm(x, axis=-1), 0.0)
    x = x + _L0_gnn_ref(h, src, dst, edge_weight, L0_gnn_weight, L0_gnn_b)
    h = jnp.maximum(_layernorm(x, axis=-1), 0.0)
    x = x + _L1_gnn_ref(h, edge_index, edge_attr_32, L1_gnn_We, L1_gnn_be, L1_gnn_W1, L1_gnn_b1, L1_gnn_W2, L1_gnn_b2)
    return x

_drawn_inputs = setup_inputs


def setup_inputs(seed=0):
    import zlib

    import numpy as np

    out = dict(_drawn_inputs(seed))
    spreads = {'L1_gnn_be': (0.0, 0.1), 'L1_gnn_b1': (0.0, 0.8), 'L1_gnn_b2': (0.0, 0.376)}
    factors = {'edge_weight': 5.907, 'L0_gnn_b': 7.406}
    for name, (base, spread) in spreads.items():
        noise = np.random.default_rng([zlib.crc32(name.encode()), seed]).standard_normal(out[name].shape)
        drawn = base * np.exp(spread * noise) if base else spread * noise
        out[name] = jnp.asarray(drawn.astype(out[name].dtype))
    for name, factor in factors.items():
        out[name] = (out[name] * factor).astype(out[name].dtype)
    return out
```

```python
import concourse.bass as bass
from concourse import mybir
from contextlib import ExitStack


def gnn_preln_two_layers(nc, x, src, dst, edge_attr, edge_weight, w0, b0, we, be, w1, b1, w2, b2, out):
    fp32, bf16, i32 = mybir.dt.float32, mybir.dt.bfloat16, mybir.dt.int32
    ALU = mybir.AluOpType
    ACT = mybir.ActivationFunctionType
    AX = mybir.AxisListType

    N, D = x.shape
    E, ED = edge_attr.shape
    P = 128
    NP = 125
    NC = N // NP
    TILES, SECTIONS = 5, 5
    LOG_W = 5
    WINDOW = 2 ** LOG_W
    TPR = TILES * SECTIONS
    SEC_E = TILES * P
    ROUNDS = E // (TPR * P)
    RE = TPR * P
    NSEC = ROUNDS * SECTIONS
    HI = 392
    HG, HP = 4, 98
    GEN = 500
    NGEN = N // GEN
    FAR = 20000.0
    CH, CHC = 5, NC // 5
    EPS = 1e-5
    GROUP4 = 4
    assert NP * NC == N and ROUNDS * RE == E and ROUNDS <= P and NGEN * GEN == N and HP * HG * WINDOW >= N

    meta_dram = nc.dram_tensor("section_meta", (2, ROUNDS, SECTIONS), i32, kind="Internal").ap()
    deg_dram = nc.dram_tensor("degrees", (HG * HP * WINDOW,), fp32, kind="Internal").ap()
    table_dram = [nc.dram_tensor(f"table{L}", (N, D), fp32, kind="Internal").ap() for L in range(2)]

    ea_view = edge_attr.rearrange("(r s p j) d -> r s p (j d)", s=SECTIONS, p=P, j=TILES)
    ctx = ExitStack()
    with ctx:
        def sb(name, shape, dt=fp32):
            return ctx.enter_context(nc.sbuf_tensor(name, shape, dt))

        def sem(name):
            return ctx.enter_context(nc.semaphore(name))

        agg = sb("agg", [P, 4 * RE])
        dst_e = agg[0:ROUNDS, 0:RE]
        src_e = agg[0:ROUNDS, RE:2 * RE]
        wgt_e = agg[0:ROUNDS, 2 * RE:3 * RE]
        rel_e = agg[0:ROUNDS, 3 * RE:4 * RE]
        rel_b = sb("rel_b", [ROUNDS, RE], bf16)
        xres = sb("xres", [NP, NC, D])
        hbuf = sb("hbuf", [NP, NC, D])
        tbl = sb("tbl", [P, NC * D])
        tbl3 = tbl[0:NP, :].rearrange("p (c d) -> p c d", d=D)
        left = tbl[:, 0:ROUNDS * TPR].rearrange("p (r k) -> p r k", k=TPR)
        left_i = tbl[:, ROUNDS * TPR:2 * ROUNDS * TPR].rearrange("p (r k) -> p r k", k=TPR)
        idx = sb("idx", [P, ROUNDS, TPR], i32)
        rel = sb("rel", [P, ROUNDS, TPR])
        wgt = sb("wgt", [P, ROUNDS, TPR])
        stage = sb("stage", [P, SECTIONS, TILES], i32)
        g = sb("g", [P, SECTIONS, TILES, D])
        msg = sb("msg", [P, SECTIONS, TILES, D])
        oh = sb("oh", [P, SECTIONS, TILES, WINDOW])
        ea = sb("ea", [P, SECTIONS, TILES * ED])
        eaT = sb("eaT", [P, 2, 2, P])
        iota_g = sb("iota_g", [P, GEN])
        wide = sb("wide", [P, GEN])
        shift = sb("shift", [P, TPR])
        shift_lo = sb("shift_lo", [P, TPR])
        ident = sb("ident", [P, P])
        meta_row = sb("meta_row", [1, 2 * NSEC], i32)
        flag_f = sb("flag_f", [1, 1])
        flag_i = sb("flag_i", [1, 1], i32)
        lo = sb("lo", [ROUNDS, SECTIONS])
        hi = sb("hi", [ROUNDS, SECTIONS])
        meta_i = sb("meta_i", [ROUNDS, 2, SECTIONS], i32)
        block_i = sb("block_i", [ROUNDS, SECTIONS], i32)
        bl = sb("bl", [ROUNDS, SECTIONS])
        bh = sb("bh", [ROUNDS, SECTIONS])
        bit = sb("bit", [ROUNDS, SECTIONS])
        PAD = WINDOW // 2
        hist = sb("hist", [ROUNDS, SECTIONS, PAD + 2 * WINDOW])
        histd = sb("histd", [ROUNDS, SECTIONS, 2 * WINDOW])
        flat_g = g[0:ROUNDS, :, :, :].rearrange("p s j d -> p (s j d)")
        flat_msg = msg[0:ROUNDS, :, :, :].rearrange("p s j d -> p (s j d)")
        hit = ea[0:ROUNDS, 0:4, :].rearrange("p s d -> p (s d)").bitcast(bf16).rearrange("p (h e) -> p h e", h=2)

        def ohb_of(s):
            return (flat_g if s < 3 else flat_msg)[:, (s % 3) * (HI + 1):(s % 3 + 1) * (HI + 1)]

        degs = sb("degs", [HP, HG, WINDOW])
        deg = sb("deg", [NP, NC])
        norm = sb("norm", [NP, NC])
        mean = sb("mean", [NP, NC])
        rstd = sb("rstd", [NP, NC])
        w0_s = sb("w0_s", [D, D])
        w0T = sb("w0T", [D, D])
        w1_s = sb("w1_s", [D, D])
        w2_s = sb("w2_s", [D, D])
        we_s = sb("we_s", [P, TILES - 1, D])
        rows = sb("rows", [NP, 3, D])
        b1_c = sb("b1_c", [D, 1])
        zcol = sb("zcol", [P, 1])
        r1 = eaT[0:D, :, :, :].rearrange("p a b c -> p (a b c)")
        ps = ctx.enter_context(nc.psum_tensor("ps", [P, 8, 512], fp32))

        def tr_bank(s):
            return ps[:, s % 2, :]

        def mbank(s):
            return ps[:, (2, 3, 4, 5, 6)[s], 0:TILES * D]

        def win(s):
            return ps[0:D, 7, s * WINDOW:(s + 1) * WINDOW]

        ld_dst, ld_src, ld_wgt, ld_x, ld_par = sem("ld_dst"), sem("ld_src"), sem("ld_wgt"), sem("ld_x"), sem("ld_par")
        we_zeroed = sem("we_zeroed")
        consts_ready = sem("consts_ready")
        meta_ready, meta_stored, meta_loaded = sem("meta_ready"), sem("meta_stored"), sem("meta_loaded")
        rel_ready, srcf_ready = sem("rel_ready"), sem("srcf_ready")
        edge_tr, edge_ev = sem("edge_tr"), sem("edge_ev")
        hist_ready, degmm_done, degs_ready = sem("hist_ready"), sem("degmm_done"), sem("degs_ready")
        deg_stored, deg_loaded = sem("deg_stored"), sem("deg_loaded")
        agg_zeroed = sem("agg_zeroed")
        flag_ready = sem("flag_ready")
        xc_ready, sq_ready = sem("xc_ready"), sem("sq_ready")
        chunk_ready, chunk_stored = sem("chunk_ready"), sem("chunk_stored")
        var_ready, sd_ready = sem("var_ready"), sem("sd_ready")
        h_ready = sem("h_ready")
        dve_step, act_step, pool_step = sem("dve_step"), sem("act_step"), sem("pool_step")
        idx_staged, pool_turn = sem("idx_staged"), sem("pool_turn")
        gathered = [sem(f"gathered{s}") for s in range(SECTIONS)]
        onehot_ready, msg0_ready, summed, relued = sem("onehot_ready"), sem("msg0_ready"), sem("summed"), sem("relued")
        agg_done, added = sem("agg_done"), sem("added")
        ea_loaded = [sem(f"ea_loaded{s}") for s in range(SECTIONS)]
        ea_tr, ea_ev, ea_prod = sem("ea_tr"), sem("ea_ev"), sem("ea_prod")
        w0_tr, w0_ev = sem("w0_tr"), sem("w0_ev")
        mid_mm, mid_ev = sem("mid_mm"), sem("mid_ev")
        ht_mm, ht_ev = sem("ht_mm"), sem("ht_ev")
        z1_mm, z1_ev, z2_mm, z2_ev = sem("z1_mm"), sem("z1_ev"), sem("z2_mm"), sem("z2_ev")
        out_stored = sem("out_stored")
        gp_dst = sem("gp_dst")
        gp_ready = [sem(f"gp_ready{k}") for k in range(3)]
        gp_oh, gp_mm, gp_add = ([sem(f"{n}{k}") for k in range(3)] for n in ("gp_oh", "gp_mm", "gp_add"))
        gp_idx, gp_got, gp_msg = ([sem(f"{n}{k}") for k in range(2)] for n in ("gp_idx", "gp_got", "gp_msg"))
        gp_ea, gp_tr, gp_ev, gp_prod, gp_sum, gp_relu = (sem(n) for n in ("gp_ea", "gp_tr", "gp_ev", "gp_prod", "gp_sum", "gp_relu"))
        gp_step, layer_done = sem("gp_step"), sem("layer_done")
        hist_step = sem("hist_step")
        gp_row, gp_turn = sem("gp_row"), sem("gp_turn")
        gp_step2 = [sem(f"gp_shift{k}") for k in range(2)]

        def wait(eng, s, n):
            if not isinstance(n, int) or n > 0:
                eng.wait_ge(s, n)

        def linker(eng, s):
            count = [0]

            def link(ins):
                count[0] += 1
                ins.then_inc(s, 1)
                eng.wait_ge(s, count[0])
            return link

        def rounds(eng, body):
            body(0, True, False)
            with eng.Fori(1, ROUNDS - 1) as i:
                body(i, False, False)
            body(ROUNDS - 1, False, True)

        def edge_rows(a):
            return a.rearrange("(r e) -> r e", e=RE)

        EDGE_T = [(a, k, min(GROUP4, TPR - k)) for a in range(3) for k in range(0, TPR, GROUP4)]
        HT_T = NC // GROUP4
        MG = 5
        NMG = NC // MG

        block = ctx.enter_context(nc.Block())

        @block.sync
        def _(sp):
            sp.dma_start(dst_e.bitcast(i32), edge_rows(dst)).then_inc(ld_dst, 16)
            sp.dma_start(src_e.bitcast(i32), edge_rows(src)).then_inc(ld_src, 16)
            sp.dma_start(wgt_e, edge_rows(edge_weight)).then_inc(ld_wgt, 16)
            sp.dma_start(xres[:, :, :], x.rearrange("(p c) d -> p c d", c=NC)).then_inc(ld_x, 16)
            sp.dma_start(w0_s[:, :], w0).then_inc(ld_par, 16)
            sp.dma_start(w1_s[:, :], w1).then_inc(ld_par, 16)
            sp.dma_start(w2_s[:, :], w2).then_inc(ld_par, 16)
            for n, b in enumerate((b0, be, b2)):
                sp.dma_start(rows[:, n, :], b.partition_broadcast(NP)).then_inc(ld_par, 16)
            sp.dma_start(b1_c[:, :], b1.rearrange("(d o) -> d o", o=1)).then_inc(ld_par, 16)
            sp.wait_ge(we_zeroed, 1)
            for j in range(TILES - 1):
                sp.dma_start(we_s[j * ED:(j + 1) * ED, j, :], we).then_inc(ld_par, 16)
            sp.wait_ge(meta_ready, 1)
            sp.dma_start(meta_dram.rearrange("k r s -> r k s"), meta_i[:, :, :]).then_inc(meta_stored, 16)
            sp.wait_ge(meta_stored, 16)
            sp.dma_start(meta_row[:, :], meta_dram.rearrange("(o k) r s -> o (k r s)", o=1)).then_inc(meta_loaded, 16)
            sp.wait_ge(flag_ready, 1)
            far = sp.value_load(flag_i[0:1, 0:1], min_val=0, max_val=1)

            def general_dst(k, after, n):
                sp.wait_ge(after, n)
                for s in range(SECTIONS):
                    sp.dma_start(left_i[:, :, s * TILES:(s + 1) * TILES].bitcast(i32),
                                 dst.rearrange("(r s p j) -> s p r j", s=SECTIONS, p=P, j=TILES)[s]).then_inc(gp_dst, 16)

            with sp.If(far > 0):
                general_dst(0, h_ready, 1)
            sp.wait_ge(degs_ready, 1)
            sp.dma_start(deg_dram.rearrange("(g h l) -> h g l", g=HG, h=HP), degs[:, :, :]).then_inc(deg_stored, 16)
            sp.wait_ge(deg_stored, 16)
            sp.dma_start(deg[:, :], deg_dram[0:N].rearrange("(p c) -> p c", c=NC)).then_inc(deg_loaded, 16)

            def store_table(L):
                t = table_dram[L].rearrange("(p c) d -> p c d", c=NC)
                for c in range(CH):
                    sp.wait_ge(chunk_ready, L * CH + c + 1)
                    sp.dma_start(t[:, c * CHC:(c + 1) * CHC, :], tbl3[:, c * CHC:(c + 1) * CHC, :]).then_inc(chunk_stored, 16)

            store_table(0)
            with sp.If(far > 0):
                general_dst(1, chunk_stored, 16 * CH)
            store_table(1)

            def load_round(i, first, last):
                for s in range(SECTIONS):
                    if not first:
                        sp.wait_ge(ea_tr, 2 * (i * SECTIONS + s - SECTIONS + 1))
                    sp.dma_start(ea[:, s, :], ea_view[i, s]).then_inc(ea_loaded[s], 16)
            rounds(sp, load_round)
            with sp.If(far > 0):
                general_dst(2, chunk_stored, 32 * CH)
                sp.wait_ge(ea_prod, NSEC)
                with sp.Fori(0, ROUNDS) as i:
                    sp.wait_ge(gp_step, i + 1)
                    sp.dma_start(ea[:, :, :], edge_attr.rearrange("(r s p j) d -> r p s (j d)", s=SECTIONS, p=P, j=TILES)[i]).then_inc(gp_ea, 16)
            o = out.rearrange("(p c) d -> p c d", c=NC)
            for c in range(CH):
                sp.wait_ge(z2_ev, (c + 1) * CHC // GROUP4)
                sp.dma_start(o[:, c * CHC:(c + 1) * CHC, :], xres[:, c * CHC:(c + 1) * CHC, :]).then_inc(out_stored, 16)
            sp.wait_ge(out_stored, 16 * CH)

        @block.gpsimd
        def _(pool):
            link = linker(pool, pool_step)
            nc.gpsimd.memset(we_s[:, :, :], 0.0).then_inc(we_zeroed, 1)
            link(nc.gpsimd.iota(iota_g[:, :], pattern=[[1, GEN]], base=0, channel_multiplier=0,
                                allow_small_or_imprecise_dtypes=True))
            link(nc.gpsimd.memset(zcol[:, :], 0.0))
            link(nc.gpsimd.memset(ident[:, :], 0.0))
            nc.gpsimd.affine_select(out=ident[:, :], in_=ident[:, :], compare_op=ALU.not_equal, fill=1.0, base=0,
                                    pattern=[[-1, P]], channel_multiplier=1).then_inc(consts_ready, 1)
            pool.wait_ge(edge_ev, len(EDGE_T))
            pool.wait_ge(hist_ready, 1)
            nc.gpsimd.memset(agg[0:D, :], 0.0).then_inc(agg_zeroed, 1)
            pool.wait_ge(flag_ready, 1)
            far = pool.value_load(flag_i[0:1, 0:1], min_val=0, max_val=1)

            def gather(L, s, j, done):
                nc.gpsimd.indirect_dma_start(
                    out=g[:, s, j, :], out_offset=None, in_=table_dram[L][:, :],
                    in_offset=bass.IndirectOffsetOnAxis(ap=stage[:, s, j:j + 1], axis=0)).then_inc(done, 16)

            for L in range(2):
                pool.wait_ge(chunk_stored, 16 * CH * (L + 1))

                def gather_round(i, first, last):
                    for s in range(SECTIONS):
                        pool.wait_ge(idx_staged, (i + L * ROUNDS) * SECTIONS + s + 1)
                        pool.sem_inc(pool_turn, 1)
                        for j in range(TILES):
                            gather(L, s, j, gathered[s])
                rounds(pool, gather_round)
                with pool.If(far > 0):
                    with pool.Fori(0, ROUNDS) as i:
                        pool.wait_ge(gp_idx[L], i + 1)
                        pool.sem_inc(pool_turn, 1)
                        for k in range(TPR):
                            gather(L, k // TILES, k % TILES, gp_got[L])

        @block.scalar
        def _(act):
            link = linker(act, act_step)
            act.wait_ge(ld_par, 16)
            for n, (a, k, m) in enumerate(EDGE_T):
                act.wait_ge(edge_tr, n + 1)
                to = (rel, idx, wgt)[a]
                nc.scalar.copy(to[:, :, k:k + m].rearrange("p r k -> p k r"),
                               ps[:, n % 4, 0:m * ROUNDS].rearrange("p (k r) -> p k r", r=ROUNDS)).then_inc(edge_ev, 1)
            act.wait_ge(w0_tr, 1)
            nc.scalar.copy(w0T[:, :], ps[0:D, 7, 0:D]).then_inc(w0_ev, 1)

            def squares(L):
                for c in range(CH):
                    act.wait_ge(xc_ready, L * CH + c + 1)
                    nc.scalar.activation(tbl3[:, c * CHC:(c + 1) * CHC, :], hbuf[:, c * CHC:(c + 1) * CHC, :],
                                         ACT.Square).then_inc(sq_ready, 1)
                for c in range(CH):
                    cs = slice(c * CHC, (c + 1) * CHC)
                    act.wait_ge(var_ready, L * (CH + 1) + c + 1)
                    nc.scalar.activation(rstd[:, cs], rstd[:, cs], ACT.Sqrt).then_inc(sd_ready, 1)
            squares(0)
            act.wait_ge(flag_ready, 1)
            far = act.value_load(flag_i[0:1, 0:1], min_val=0, max_val=1)
            act.wait_ge(var_ready, CH + 1)
            nc.scalar.activation(norm[:, :], norm[:, :], ACT.Sqrt).then_inc(sd_ready, 1)
            act.wait_ge(chunk_stored, 16 * CH)
            squares(1)
            aggc = agg[0:D, 0:N].rearrange("f (p c) -> f c p", c=NC)
            for n in range(HT_T):
                act.wait_ge(ht_mm, n + 1)
                nc.scalar.copy(aggc[:, n * GROUP4:(n + 1) * GROUP4, :],
                               ps[0:D, n % 4, 0:GROUP4 * NP].rearrange("f (c p) -> f c p", p=NP)).then_inc(ht_ev, 1)

            def evacuate(q, s, trd, evd, slot):
                t = tr_bank(s)
                act.wait_ge(trd, 2 * q + 2)
                nc.scalar.copy(eaT[:, slot, 0, :], t[:, 0:P]).then_inc(evd, 1)
                nc.scalar.copy(eaT[0:ED, slot, 1, :], t[0:ED, P:2 * P]).then_inc(evd, 1)

            evacuate(0, 0, ea_tr, ea_ev, 0)

            def act_round(i, first, last):
                for s in range(SECTIONS):
                    q = i * SECTIONS + s
                    if not (last and s == SECTIONS - 1):
                        act.wait_ge(ea_prod, q + 1)
                        evacuate(q + 1, (s + 1) % SECTIONS, ea_tr, ea_ev, ((s + 1) % SECTIONS) % 2)
                    act.wait_ge(summed, q + 1)
                    nc.scalar.activation(msg[:, s, :, :], msg[:, s, :, :], ACT.Relu).then_inc(relued, 1)
            rounds(act, act_round)
            with act.If(far > 0):
                with act.Fori(0, ROUNDS) as i:
                    for s in range(SECTIONS):
                        q = i * SECTIONS + s
                        evacuate(q, s, gp_tr, gp_ev, s % 2)
                        act.wait_ge(gp_sum, q + 1)
                        nc.scalar.activation(msg[:, s, :, :], msg[:, s, :, :], ACT.Relu).then_inc(gp_relu, 1)
            for n in range(NC // GROUP4):
                act.wait_ge(z1_mm, n + 1)
                if n >= 1:
                    act.wait_ge(z2_mm, n)
                nc.scalar.activation(r1[:, 0:GROUP4 * NP], ps[0:D, n % 2, 0:GROUP4 * NP], ACT.Relu,
                                     bias=b1_c[:, 0:1]).then_inc(z1_ev, 1)

        @block.vector
        def _(dve):
            link = linker(dve, dve_step)

            def mul(o, a, b, op=ALU.mult):
                return nc.vector.tensor_tensor(o, a, b, op)

            dve.wait_ge(ld_dst, 16)
            link(nc.vector.tensor_copy(dst_e, dst_e.bitcast(i32)))
            ds3 = dst_e.rearrange("r (s e) -> r s e", s=SECTIONS)
            rel3 = rel_e.rearrange("r (s e) -> r s e", s=SECTIONS)
            link(nc.vector.tensor_reduce(lo[:, :], ds3, AX.X, ALU.min))
            link(mul(rel3, ds3, lo[:, :].unsqueeze(2).to_broadcast([ROUNDS, SECTIONS, SEC_E]), ALU.subtract))
            nc.vector.tensor_copy(rel_b[:, :], rel_e).then_inc(rel_ready, 1)
            nc.vector.tensor_reduce(hi[:, :], rel3, AX.X, ALU.max).then_inc(rel_ready, 1)
            dve.wait_ge(rel_ready, 2)
            nc.vector.tensor_copy(meta_i[:, 0, :], lo[:, :])
            link(nc.vector.tensor_copy(meta_i[:, 1, :], hi[:, :]))
            dve.sem_inc(meta_ready, 1)
            dve.wait_ge(ld_src, 16)
            nc.vector.tensor_copy(src_e, src_e.bitcast(i32)).then_inc(srcf_ready, 1)

            dve.wait_ge(ld_x, 16)

            def centre(L, c):
                cs = slice(c * CHC, (c + 1) * CHC)
                link(nc.vector.tensor_reduce(mean[:, cs], xres[:, cs, :], AX.X, ALU.add))
                link(nc.vector.tensor_scalar(mean[:, cs], mean[:, cs], 1.0 / D, None, ALU.mult))
                mul(hbuf[:, cs, :], xres[:, cs, :], mean[:, cs].unsqueeze(2).to_broadcast([NP, CHC, D]),
                    ALU.subtract).then_inc(xc_ready, 1)

            def variance(L, c):
                cs = slice(c * CHC, (c + 1) * CHC)
                dve.wait_ge(sq_ready, L * CH + c + 1)
                link(nc.vector.tensor_reduce(rstd[:, cs], tbl3[:, cs, :], AX.X, ALU.add))
                nc.vector.tensor_scalar(rstd[:, cs], rstd[:, cs], 1.0 / D, EPS, ALU.mult, ALU.add).then_inc(var_ready, 1)

            def normed(L, c):
                cs = slice(c * CHC, (c + 1) * CHC)
                dve.wait_ge(sd_ready, L * (CH + 1) + c + 1)
                link(nc.vector.reciprocal(rstd[:, cs], rstd[:, cs]))
                link(nc.vector.scalar_tensor_tensor(hbuf[:, cs, :], hbuf[:, cs, :], 0.0,
                                                    rstd[:, cs].unsqueeze(2).to_broadcast([NP, CHC, D]), ALU.max, ALU.mult))

            for c in range(CH):
                centre(0, c)
            for c in range(CH):
                variance(0, c)
            for c in range(CH):
                normed(0, c)
            dve.sem_inc(h_ready, 1)

            dve.wait_ge(meta_loaded, 16)
            link(nc.vector.tensor_reduce(flag_f[:, :], meta_row[:, NSEC:2 * NSEC], AX.X, ALU.max))
            link(nc.vector.tensor_scalar(flag_f[:, :], flag_f[:, :], float(WINDOW), None, ALU.is_ge))
            nc.vector.tensor_copy(flag_i[:, :], flag_f[:, :]).then_inc(flag_ready, 1)

            dve.wait_ge(consts_ready, 1)
            link(nc.vector.memset(hist[:, :, :], 0.0))
            for s in range(SECTIONS):
                for w in range(WINDOW):
                    n = s * WINDOW + w
                    wait(dve, hist_step, n - 1)
                    nc.vector.tensor_scalar(hit[:, n % 2, :], rel_b[:, s * SEC_E:(s + 1) * SEC_E], float(w), 0.0,
                                            ALU.is_equal, ALU.add,
                                            accum_out=hist[:, s, PAD + w:PAD + w + 1]).then_inc(hist_step, 1)
            dve.wait_ge(hist_step, SECTIONS * WINDOW)
            link(nc.vector.tensor_scalar(block_i[:, :], meta_i[:, 0, :], LOG_W, None, ALU.arith_shift_right))
            link(nc.vector.tensor_copy(bh[:, :], block_i[:, :]))
            link(nc.vector.scalar_tensor_tensor(bl[:, :], bh[:, :], -float(WINDOW), lo[:, :], ALU.mult, ALU.add))
            sh = PAD
            while sh:
                link(nc.vector.tensor_scalar(bit[:, :], bl[:, :], float(sh), None, ALU.is_ge))
                link(nc.vector.scalar_tensor_tensor(bl[:, :], bit[:, :], -float(sh), bl[:, :], ALU.mult, ALU.add))
                h0 = hist[:, :, PAD:PAD + 2 * WINDOW]
                link(mul(histd[:, :, :], hist[:, :, PAD - sh:PAD - sh + 2 * WINDOW], h0, ALU.subtract))
                link(mul(histd[:, :, :], histd[:, :, :],
                         bit[:, :].unsqueeze(2).to_broadcast([ROUNDS, SECTIONS, 2 * WINDOW])))
                link(mul(h0, h0, histd[:, :, :], ALU.add))
                sh //= 2
            for s in range(SECTIONS):
                o = ohb_of(s)
                nc.vector.memset(o[:, 0:1], 0.0)
                link(nc.vector.tensor_scalar(o[:, 1:HI + 1], iota_g[0:ROUNDS, 0:HI], bh[:, s:s + 1], None, ALU.is_equal))
            dve.sem_inc(hist_ready, 1)
            dve.wait_ge(degmm_done, 1)
            link(nc.vector.tensor_copy(degs[:, :, :].rearrange("h g l -> h (g l)"), ps[0:HP, 6, 0:HG * WINDOW]))
            far = dve.value_load(flag_i[0:1, 0:1], min_val=0, max_val=1)

            def far_edges(k):
                dve.wait_ge(gp_dst, 16 * SECTIONS * (k + 1))
                nc.vector.tensor_copy(left, left_i.bitcast(i32)).then_inc(gp_ready[k], 1)
                dve.wait_ge(gp_ready[k], 1)
                nc.vector.tensor_scalar(left, left, FAR, None, ALU.subtract).then_inc(gp_ready[k], 1)
                nc.vector.tensor_scalar(left_i, rel[:, :, :], float(WINDOW), None, ALU.is_ge).then_inc(gp_ready[k], 1)
                dve.wait_ge(gp_ready[k], 3)
                mul(left, left, left_i).then_inc(gp_ready[k], 1)
                dve.wait_ge(gp_ready[k], 4)
                nc.vector.tensor_scalar(left, left, FAR, None, ALU.add).then_inc(gp_ready[k], 1)
                dve.wait_ge(gp_ready[k], 5)

            with dve.If(far > 0):
                far_edges(0)
                nc.vector.tensor_copy(left_i.bitcast(i32), left).then_inc(gp_ready[0], 1)
                dve.wait_ge(gp_ready[0], 6)
                nc.vector.tensor_scalar(left_i.bitcast(i32), left_i.bitcast(i32), LOG_W, None,
                                        ALU.arith_shift_right).then_inc(gp_ready[0], 1)
                dve.wait_ge(gp_ready[0], 7)
                nc.vector.tensor_copy(left_i, left_i.bitcast(i32)).then_inc(gp_ready[0], 1)
                dve.wait_ge(gp_ready[0], 8)
                nc.vector.scalar_tensor_tensor(left, left_i, -float(WINDOW), left, ALU.mult, ALU.add).then_inc(gp_ready[0], 1)
                dve.wait_ge(gp_ready[0], 9)
                with dve.Fori(0, ROUNDS) as i:
                    nc.vector.tensor_copy(shift[:, :], left_i[:, bass.ds(i, 1), :].rearrange("p o k -> p (o k)")).then_inc(gp_row, 1)
                    nc.vector.tensor_copy(shift_lo[:, :], left[:, bass.ds(i, 1), :].rearrange("p o k -> p (o k)")).then_inc(gp_row, 1)
                    dve.wait_ge(gp_row, 2 * (i + 1))
                    for k in range(TPR):
                        n = i * TPR + k
                        nc.vector.tensor_scalar(wide[:, 0:HI], iota_g[:, 0:HI], shift[:, k:k + 1], None,
                                                ALU.is_equal).then_inc(gp_oh[0], 1)
                        nc.vector.tensor_scalar(oh[:, 0, 0, :], iota_g[:, 0:WINDOW], shift_lo[:, k:k + 1], None,
                                                ALU.is_equal).then_inc(gp_oh[0], 1)
                        dve.wait_ge(gp_mm[0], n + 1)
                        mul(degs[:, :, :].rearrange("h g l -> h (g l)"), degs[:, :, :].rearrange("h g l -> h (g l)"),
                            ps[0:HP, 5, 0:HG * WINDOW], ALU.add).then_inc(gp_add[0], 1)
                        dve.wait_ge(gp_add[0], n + 1)
            dve.sem_inc(degs_ready, 1)
            dve.wait_ge(deg_loaded, 16)
            nc.vector.tensor_scalar(norm[:, :], deg[:, :], 1.0, None, ALU.max).then_inc(var_ready, 1)
            dve.wait_ge(sd_ready, CH + 1)
            link(nc.vector.reciprocal(norm[:, :], norm[:, :]))
            link(nc.vector.tensor_scalar(deg[:, :], deg[:, :], 0.0, None, ALU.is_gt))
            link(mul(norm[:, :], norm[:, :], deg[:, :]))
            for c in range(CH):
                cs = slice(c * CHC, (c + 1) * CHC)
                mul(tbl3[:, cs, :], hbuf[:, cs, :],
                    norm[:, cs].unsqueeze(2).to_broadcast([NP, CHC, D])).then_inc(chunk_ready, 1)
            dve.wait_ge(ld_par, 16 * 11)
            link(mul(xres[:, :, :], xres[:, :, :], rows[:, 0, :].unsqueeze(1).to_broadcast([NP, NC, D]), ALU.add))

            def stage_round(i, s, count):
                nc.vector.tensor_copy(stage[:, s:s + 1, :], idx[:, bass.ds(i, 1), s * TILES:(s + 1) * TILES] if not isinstance(i, int)
                                      else idx[:, i:i + 1, s * TILES:(s + 1) * TILES]).then_inc(idx_staged, 1)

            dve.wait_ge(edge_ev, len(EDGE_T))
            for s in range(SECTIONS):
                stage_round(0, s, s)
            dve.wait_ge(agg_zeroed, 1)

            def one(i):
                return bass.ds(i, 1) if not isinstance(i, int) else slice(i, i + 1)

            def layer(L):
                def dve_round(i, first, last):
                    for s in range(SECTIONS):
                        q = i * SECTIONS + s
                        Q = q + L * NSEC
                        ks = slice(s * TILES, (s + 1) * TILES)
                        base = dve.value_load(meta_row[0:1, bass.ds(q, 1) if not isinstance(q, int) else slice(q, q + 1)],
                                              min_val=0, max_val=N - 1)
                        mul(oh[:, s, :, :], iota_g[:, 0:WINDOW].unsqueeze(1).to_broadcast([P, TILES, WINDOW]),
                            rel[:, one(i), ks].rearrange("p o k -> p (o k)").unsqueeze(2).to_broadcast([P, TILES, WINDOW]),
                            ALU.is_equal).then_inc(onehot_ready, 1)
                        dve.wait_ge(gathered[s], (i + L * ROUNDS + 1) * 16 * TILES)
                        if L == 0:
                            mul(msg[:, s, :, :], g[:, s, :, :],
                                wgt[:, one(i), ks].rearrange("p o k -> p (o k)").unsqueeze(2).to_broadcast([P, TILES, D])
                                ).then_inc(msg0_ready, 1)
                            dve.wait_ge(msg0_ready, q + 1)
                        else:
                            dve.wait_ge(ea_prod, q + 1)
                            mul(msg[:, s, :, :], mbank(s).rearrange("p (j d) -> p j d", d=D), g[:, s, :, :],
                                ALU.add).then_inc(summed, 1)
                            dve.wait_ge(summed, q + 1)
                        if not last:
                            stage_round(i + 1, s, 0)
                        elif L == 0:
                            stage_round(0, s, 0)
                        dve.wait_ge(agg_done, Q + 1)
                        wait(dve, added, Q)
                        a = agg[0:D, bass.ds(base, WINDOW)]
                        mul(a, a, win(s), ALU.add).then_inc(added, 1)
                rounds(dve, dve_round)
                dve.wait_ge(added, NSEC * (L + 1))
                with dve.If(far > 0):
                    far_edges(L + 1)
                    with dve.Fori(0, ROUNDS) as i:
                        nc.vector.tensor_copy(shift[:, :], left[:, bass.ds(i, 1), :].rearrange("p o k -> p (o k)")).then_inc(gp_step2[L], 1)
                        nc.vector.tensor_copy(stage[:, :, :].rearrange("p s j -> p (s j)"),
                                              idx[:, bass.ds(i, 1), :].rearrange("p o k -> p (o k)")).then_inc(gp_idx[L], 1)
                        dve.wait_ge(gp_got[L], (i + 1) * 16 * TPR)
                        if L == 0:
                            mul(msg[:, :, :, :].rearrange("p s j d -> p (s j) d"), g[:, :, :, :].rearrange("p s j d -> p (s j) d"),
                                wgt[:, bass.ds(i, 1), :].rearrange("p o k -> p (o k)").unsqueeze(2).to_broadcast([P, TPR, D])
                                ).then_inc(gp_msg[0], 1)
                        else:
                            for s in range(SECTIONS):
                                dve.wait_ge(gp_prod, i * SECTIONS + s + 1)
                                mul(msg[:, s, :, :], mbank(s).rearrange("p (j d) -> p j d", d=D), g[:, s, :, :],
                                    ALU.add).then_inc(gp_sum, 1)
                        with dve.Fori(0, NGEN) as v:
                            for k in range(TPR):
                                n = (i * NGEN + v) * TPR + k
                                if k == 0:
                                    dve.wait_ge(gp_step2[L], i * (NGEN + 1) + v + 1)
                                nc.vector.tensor_scalar(wide[:, :], iota_g[:, :], shift[:, k:k + 1], None,
                                                        ALU.is_equal).then_inc(gp_oh[L + 1], 1)
                                dve.wait_ge(gp_mm[L + 1], n + 1)
                            nc.vector.tensor_scalar(shift[:, :], shift[:, :], float(GEN), None, ALU.subtract).then_inc(gp_step2[L], 1)
                            a = agg[0:D, bass.ds(v * GEN, GEN)]
                            mul(a, a, ps[0:D, 7, 0:GEN], ALU.add).then_inc(gp_add[L + 1], 1)
                            dve.wait_ge(gp_add[L + 1], i * NGEN + v + 1)
                dve.sem_inc(layer_done, 1)

            layer(0)
            for n in range(NMG):
                cs = slice(n * MG, (n + 1) * MG)
                dve.wait_ge(mid_mm, n + 1)
                mul(hbuf[:, cs, :], ps[0:NP, n % 4, 0:MG * D].rearrange("p (c d) -> p c d", d=D),
                    norm[:, cs].unsqueeze(2).to_broadcast([NP, MG, D])).then_inc(mid_ev, 1)
                dve.wait_ge(mid_ev, n + 1)
                link(mul(xres[:, cs, :], xres[:, cs, :], hbuf[:, cs, :], ALU.add))
                if (n + 1) * MG % CHC == 0:
                    centre(1, (n + 1) * MG // CHC - 1)
            for c in range(CH):
                variance(1, c)
            for c in range(CH):
                normed(1, c)
                cs = slice(c * CHC, (c + 1) * CHC)
                mul(tbl3[:, cs, :], hbuf[:, cs, :], rows[:, 1, :].unsqueeze(1).to_broadcast([NP, CHC, D]),
                    ALU.add).then_inc(chunk_ready, 1)
            dve.sem_inc(h_ready, 1)
            link(mul(xres[:, :, :], xres[:, :, :], rows[:, 2, :].unsqueeze(1).to_broadcast([NP, NC, D]), ALU.add))
            dve.wait_ge(ht_ev, HT_T)
            layer(1)
            for n in range(NC // GROUP4):
                cs = slice(n * GROUP4, (n + 1) * GROUP4)
                dve.wait_ge(z2_mm, n + 1)
                mul(xres[:, cs, :], xres[:, cs, :],
                    ps[0:NP, 2 + n % 2, 0:GROUP4 * D].rearrange("p (c d) -> p c d", d=D), ALU.add).then_inc(z2_ev, 1)

        @block.tensor
        def _(pe):
            pe.wait_ge(consts_ready, 1)
            pe.wait_ge(ld_par, 16 * 11)
            nc.tensor.transpose(ps[0:D, 7, 0:D], w0_s[:, :], ident[0:D, 0:D]).then_inc(w0_tr, 1)
            for n, (a, k, m) in enumerate(EDGE_T):
                if k == 0:
                    if a == 0:
                        pe.wait_ge(rel_ready, 2)
                    elif a == 1:
                        pe.wait_ge(srcf_ready, 1)
                    else:
                        pe.wait_ge(ld_wgt, 16)
                if n >= 4:
                    pe.wait_ge(edge_ev, n - 3)
                arr = (rel_e, src_e, wgt_e)[a].rearrange("r (s p j) -> r s j p", s=SECTIONS, p=P)
                for t in range(m):
                    last = nc.tensor.transpose(ps[:, n % 4, t * ROUNDS:(t + 1) * ROUNDS],
                                               arr[:, (k + t) // TILES, (k + t) % TILES, :], ident[0:ROUNDS, 0:ROUNDS])
                last.then_inc(edge_tr, 1)
            pe.wait_ge(hist_ready, 1)
            for gp in range(HG):
                steps = [(s, half) for s in range(SECTIONS) for half in range(2)]
                for n, (s, half) in enumerate(steps):
                    o = ohb_of(s)
                    last = nc.tensor.matmul(ps[0:HP, 6, gp * WINDOW:(gp + 1) * WINDOW],
                                            o[:, 1 - half + gp * HP:1 - half + (gp + 1) * HP],
                                            hist[:, s, PAD + half * WINDOW:PAD + (half + 1) * WINDOW],
                                            start=(n == 0), stop=(n == len(steps) - 1))
            last.then_inc(degmm_done, 1)
            pe.wait_ge(flag_ready, 1)
            far = pe.value_load(flag_i[0:1, 0:1], min_val=0, max_val=1)
            with pe.If(far > 0):
                with pe.Fori(0, ROUNDS) as i:
                    for k in range(TPR):
                        pe.wait_ge(gp_oh[0], 2 * (i * TPR + k + 1))
                        for gp in range(HG):
                            last = nc.tensor.matmul(ps[0:HP, 5, gp * WINDOW:(gp + 1) * WINDOW],
                                                    wide[:, gp * HP:(gp + 1) * HP], oh[:, 0, 0, :], start=True, stop=True)
                        last.then_inc(gp_mm[0], 1)

            def transposes(s, done):
                t = tr_bank(s)
                cut = (TILES - 1) * ED
                nc.tensor.transpose(t[:, 0:P], ea[:, s, 0:cut], ident[:, :]).then_inc(done, 1)
                nc.tensor.transpose(t[0:ED, P:2 * P], ea[:, s, cut:cut + ED], ident[:, :]).then_inc(done, 1)

            def products(s, done):
                nc.tensor.matmul(mbank(s)[:, 0:(TILES - 1) * D], eaT[:, s % 2, 0, :],
                                 we_s[:, :, :].rearrange("p j d -> p (j d)"), start=True, stop=True)
                last = nc.tensor.matmul(mbank(s)[:, (TILES - 1) * D:], eaT[0:ED, s % 2, 1, :], we_s[0:ED, 0, :],
                                        start=True, stop=True)
                last.then_inc(done, 1)

            def window_sums(s):
                for j in range(TILES):
                    last = nc.tensor.matmul(win(s), msg[:, s, j, :], oh[:, s, j, :], start=(j == 0), stop=(j == TILES - 1))
                last.then_inc(agg_done, 1)

            def attributes(q, s, i):
                pe.wait_ge(ea_loaded[s], 16 * (i + 1))
                transposes(s, ea_tr)
                pe.wait_ge(ea_ev, 2 * (q + 1))
                products(s, ea_prod)

            for L in range(2):
                if L == 1:
                    attributes(0, 0, 0)

                def pe_round(i, first, last):
                    for s in range(SECTIONS):
                        q = i * SECTIONS + s
                        if L == 1 and not (last and s == SECTIONS - 1):
                            attributes(q + 1, (s + 1) % SECTIONS, i + (1 if s == SECTIONS - 1 else 0))
                        pe.wait_ge(onehot_ready, q + L * NSEC + 1)
                        pe.wait_ge(relued if L else msg0_ready, q + 1)
                        window_sums(s)
                rounds(pe, pe_round)
                with pe.If(far > 0):
                    with pe.Fori(0, ROUNDS) as i:
                        if L == 0:
                            pe.wait_ge(gp_msg[0], i + 1)
                        else:
                            pe.sem_inc(gp_step, 1)
                            pe.wait_ge(gp_ea, 16 * (i + 1))
                            for s in range(SECTIONS):
                                transposes(s, gp_tr)
                                pe.wait_ge(gp_ev, 2 * (i * SECTIONS + s + 1))
                                products(s, gp_prod)
                                pe.wait_ge(gp_relu, i * SECTIONS + s + 1)
                        pe.sem_inc(gp_turn, 1)
                        with pe.Fori(0, NGEN) as v:
                            for k in range(TPR):
                                pe.wait_ge(gp_oh[L + 1], (i * NGEN + v) * TPR + k + 1)
                                nc.tensor.matmul(ps[0:D, 7, 0:GEN], msg[:, k // TILES, k % TILES, :], wide[:, :],
                                                 start=(k == 0), stop=(k == TPR - 1)).then_inc(gp_mm[L + 1], 1)
                pe.wait_ge(layer_done, L + 1)
                aggc = agg[0:D, 0:N].rearrange("f (p c) -> f c p", c=NC)
                if L == 0:
                    pe.wait_ge(w0_ev, 1)
                    for n in range(NMG):
                        if n >= 4:
                            pe.wait_ge(mid_ev, n - 3)
                        for c in range(MG):
                            last = nc.tensor.matmul(ps[0:NP, n % 4, c * D:(c + 1) * D], aggc[:, n * MG + c, :],
                                                    w0T[:, :], start=True, stop=True)
                        last.then_inc(mid_mm, 1)
                    pe.wait_ge(h_ready, 2)
                    for n in range(HT_T):
                        if n >= 4:
                            pe.wait_ge(ht_ev, n - 3)
                        for c in range(GROUP4):
                            last = nc.tensor.transpose(ps[0:D, n % 4, c * NP:(c + 1) * NP], hbuf[:, n * GROUP4 + c, :],
                                                       ident[0:NP, 0:NP])
                        last.then_inc(ht_mm, 1)
                    pe.wait_ge(ht_ev, HT_T)
                else:
                    def first_product(n):
                        if n >= 2:
                            pe.wait_ge(z1_ev, n - 1)
                        nc.tensor.matmul(ps[0:D, n % 2, 0:GROUP4 * NP], w1_s[:, :],
                                         aggc[:, n * GROUP4:(n + 1) * GROUP4, :], start=True, stop=True).then_inc(z1_mm, 1)
                    first_product(0)
                    for n in range(NC // GROUP4):
                        if n + 1 < NC // GROUP4:
                            first_product(n + 1)
                        pe.wait_ge(z1_ev, n + 1)
                        if n >= 2:
                            pe.wait_ge(z2_ev, n - 1)
                        for c in range(GROUP4):
                            last = nc.tensor.matmul(ps[0:NP, 2 + n % 2, c * D:(c + 1) * D], r1[:, c * NP:(c + 1) * NP],
                                                    w2_s[:, :], start=True, stop=True)
                        last.then_inc(z2_mm, 1)


_INS = ['x', 'src', 'dst', 'edge_attr_32', 'edge_weight', 'L0_gnn_weight', 'L0_gnn_b', 'L1_gnn_We', 'L1_gnn_be',
        'L1_gnn_W1', 'L1_gnn_b1', 'L1_gnn_W2', 'L1_gnn_b2']


def kernel(**inputs):
    import numpy as _np
    import concourse.bacc as _bacc
    from concourse import mybir as _mybir
    from concourse.bass_utils import run_bass_kernel_spmd as _run

    nc = _bacc.Bacc("TRN2", target_bir_lowering=False, num_devices=1)
    arrays, args = {}, []
    for name in _INS:
        a = _np.ascontiguousarray(inputs[name])
        arrays[f"in_{name}_dram"] = a
        args.append(nc.dram_tensor(f"in_{name}_dram", a.shape, _mybir.dt.from_np(a.dtype), kind="ExternalInput").ap())
    out = nc.dram_tensor("out_0_dram", inputs['x'].shape, _mybir.dt.float32, kind="ExternalOutput").ap()
    gnn_preln_two_layers(nc, *args, out)
    r = _run(nc, [arrays], core_ids=[0])
    return r.results[0]["out_0_dram"]
```

```python
import concourse.bass as bass
from concourse import mybir
from contextlib import ExitStack


def gnn_preln_two_layers(nc, x, src, dst, edge_attr, edge_weight, w0, b0, we, be, w1, b1, w2, b2, out):
    fp32, fp16, bf16, i32 = mybir.dt.float32, mybir.dt.float16, mybir.dt.bfloat16, mybir.dt.int32
    ALU = mybir.AluOpType
    ACT = mybir.ActivationFunctionType
    AX = mybir.AxisListType

    N, D = x.shape
    E, ED = edge_attr.shape
    P = 128
    NP = 125
    NC = N // NP
    TILES, SECTIONS = 5, 5
    LOG_W = 5
    WINDOW = 2 ** LOG_W
    TPR = TILES * SECTIONS
    SEC_E = TILES * P
    ROUNDS = E // (TPR * P)
    RE = TPR * P
    NSEC = ROUNDS * SECTIONS
    HI = 392
    HG, HP = 4, 98
    GEN = 500
    NGEN = N // GEN
    FAR = 20000.0
    CH, CHC = 10, NC // 10
    EPS = 1e-5
    MG = 5
    LOADS = 2 + 2 + 2 + TILES + 2 + TILES - 1
    GROUP4 = 4
    W_ACT = 23
    assert NP * NC == N and ROUNDS * RE == E and ROUNDS <= P and NGEN * GEN == N and HP * HG * WINDOW >= N

    meta_dram = nc.dram_tensor("section_meta", (NSEC + ROUNDS,), i32, kind="Internal").ap()
    deg_dram = nc.dram_tensor("degrees", (HG * HP * WINDOW,), fp32, kind="Internal").ap()
    table_dram = [nc.dram_tensor(f"table{L}", (N, D), fp32, kind="Internal").ap() for L in range(2)]

    ea_view = edge_attr.rearrange("(r s p j) d -> r s p (j d)", s=SECTIONS, p=P, j=TILES)
    ctx = ExitStack()
    with ctx:
        def sb(name, shape, dt=fp32):
            return ctx.enter_context(nc.sbuf_tensor(name, shape, dt))

        def sem(name):
            return ctx.enter_context(nc.semaphore(name))

        agg = sb("agg", [P, 4 * RE])
        dst_e = agg[0:ROUNDS, 0:RE]
        src_e = agg[0:ROUNDS, RE:2 * RE]
        wgt_e = agg[0:ROUNDS, 2 * RE:3 * RE]
        rel_e = agg[0:ROUNDS, 3 * RE:4 * RE]
        rel_b = sb("rel_b", [ROUNDS, RE], bf16)
        xres = sb("xres", [NP, NC, D])
        hbuf = sb("hbuf", [NP, NC, D])
        tbl = sb("tbl", [P, NC * D])
        tbl3 = tbl[0:NP, :].rearrange("p (c d) -> p c d", d=D)
        left = tbl[:, 0:ROUNDS * TPR].rearrange("p (r k) -> p r k", k=TPR)
        left_i = tbl[:, ROUNDS * TPR:2 * ROUNDS * TPR].rearrange("p (r k) -> p r k", k=TPR)
        idx = sb("idx", [P, ROUNDS, TPR])
        relw = sb("relw", [P, ROUNDS, 2, TPR])
        rel, wgt = relw[:, :, 0, :], relw[:, :, 1, :]
        stage = sb("stage", [P, SECTIONS, TILES], i32)
        cols = sb("cols", [P, SECTIONS, 2, TILES])
        g = sb("g", [P, SECTIONS, TILES, D])
        msg = sb("msg", [P, SECTIONS, TILES, D])
        oh = sb("oh", [P, SECTIONS, TILES, WINDOW])
        ea = sb("ea", [P, SECTIONS, TILES * ED])
        eaT = sb("eaT", [P, 2, 2, P])
        iota_g = sb("iota_g", [P, GEN])
        wide = sb("wide", [P, GEN])
        shift = sb("shift", [P, TPR])
        shift_lo = sb("shift_lo", [P, TPR])
        ident = sb("ident", [P, P])
        meta_row = sb("meta_row", [1, NSEC + ROUNDS], i32)
        flag_f = sb("flag_f", [1, 1])
        flag_i = sb("flag_i", [1, 1], i32)
        lo = sb("lo", [ROUNDS, SECTIONS])
        meta_i = sb("meta_i", [ROUNDS, SECTIONS], i32)
        over = sb("over", [ROUNDS, 1])
        block_i = sb("block_i", [ROUNDS, SECTIONS], i32)
        bl = sb("bl", [ROUNDS, SECTIONS])
        bh = sb("bh", [ROUNDS, SECTIONS])
        bits = sb("bits", [ROUNDS, LOG_W, SECTIONS])
        bit_step = sb("bit_step", [ROUNDS, SECTIONS])
        PAD = WINDOW // 2
        assert SEC_E <= 2048
        hist = sb("hist", [ROUNDS, SECTIONS, PAD + 2 * WINDOW], fp16)
        histd = sb("histd", [ROUNDS, SECTIONS, 2 * WINDOW], fp16)
        signs = sb("signs", [ROUNDS, SECTIONS, WINDOW + 1 - W_ACT])
        half_off = sb("half_off", [P, WINDOW + 1])
        flat_msg = msg[0:ROUNDS, :, :, :].rearrange("p s j d -> p (s j d)").bitcast(fp16)
        hit = ea[0:ROUNDS, 0:4, :].rearrange("p s d -> p (s d)").bitcast(bf16).rearrange("p (h e) -> p h e", h=2)
        hit_act = g[0:ROUNDS, :, :, :].rearrange("p s j d -> p (s j d)").bitcast(bf16)[:, 0:RE]

        def ohb_of(s):
            return flat_msg[:, s * (HI + 2):s * (HI + 2) + HI + 1]

        degs = sb("degs", [HP, HG, WINDOW])
        scratch = msg[0:NP, :, :, :].rearrange("p s j d -> p (s j d)")[:, 0:2 * MG * (D + 1)].rearrange(
            "p (n c d) -> p n c d", n=2, c=MG)
        deg = sb("deg", [NP, NC])
        norm = sb("norm", [NP, NC])
        mean = sb("mean", [NP, NC])
        rstd = sb("rstd", [NP, NC])
        w0_s = sb("w0_s", [D, D])
        w0T = sb("w0T", [D, D + 1])
        w1_s = sb("w1_s", [D, D])
        w2_s = sb("w2_s", [2 * D, 2, D])
        be_row = sb("be_row", [1, TILES, D])
        ones = sb("ones", [1, P])
        we_s = sb("we_s", [P, TILES - 1, D])
        rows = sb("rows", [NP, 2, D])
        b0_mean = sb("b0_mean", [NP, 1])
        b1_c = sb("b1_c", [2 * D, 1])

        r1 = eaT[:, :, :, :].rearrange("p a b c -> p (a b c)")
        ps = ctx.enter_context(nc.psum_tensor("ps", [P, 8, 512], fp32))

        def tr_bank(s):
            return ps[:, s % 2, :]

        def mbank(s):
            return ps[:, 2 + s % 3, 0:TILES * D]

        def win(s):
            return ps[0:D, 7, s * WINDOW:(s + 1) * WINDOW]

        iota_p = ps[:, 5, 0:WINDOW]

        ld_dst, ld_src, ld_wgt, ld_x, ld_par = sem("ld_dst"), sem("ld_src"), sem("ld_wgt"), sem("ld_x"), sem("ld_par")
        diag_zeroed = sem("diag_zeroed")
        consts_ready = sem("consts_ready")
        meta_ready, meta_stored, meta_loaded = sem("meta_ready"), sem("meta_stored"), sem("meta_loaded")
        rel_ready, srcf_ready = sem("rel_ready"), sem("srcf_ready")
        edge_tr, edge_ev = sem("edge_tr"), sem("edge_ev")
        hist_ready, degmm_done, degs_ready = sem("hist_ready"), sem("degmm_done"), sem("degs_ready")
        deg_stored, deg_loaded = sem("deg_stored"), sem("deg_loaded")
        agg_zeroed = sem("agg_zeroed")
        flag_ready = sem("flag_ready")
        xc_ready, sq_ready = sem("xc_ready"), sem("sq_ready")
        chunk_ready, chunk_stored = sem("chunk_ready"), sem("chunk_stored")
        var_ready, sd_ready = sem("var_ready"), sem("sd_ready")
        dve_step, act_step, pool_step = sem("dve_step"), sem("act_step"), sem("pool_step")
        idx_staged, pool_turn = sem("idx_staged"), sem("pool_turn")
        gathered = [sem(f"gathered{s}") for s in range(SECTIONS)]
        cols_staged, act_turn = sem("cols_staged"), sem("act_turn")
        onehot_ready, summed, relued = sem("onehot_ready"), sem("summed"), sem("relued")
        agg_done, added = sem("agg_done"), sem("added")
        ea_loaded = [sem(f"ea_loaded{s}") for s in range(SECTIONS)]
        ea_tr, ea_ev, ea_prod = sem("ea_tr"), sem("ea_ev"), sem("ea_prod")
        w0_tr, w0_ev = sem("w0_tr"), sem("w0_ev")
        mid_mm, mid_ev = sem("mid_mm"), sem("mid_ev")
        ht_mm, ht_ev = sem("ht_mm"), sem("ht_ev")
        z1_mm, z1_ev, z2_mm, z2_ev = sem("z1_mm"), sem("z1_ev"), sem("z2_mm"), sem("z2_ev")
        out_stored = sem("out_stored")
        gp_dst = sem("gp_dst")
        gp_ready = [sem(f"gp_ready{k}") for k in range(3)]
        gp_oh, gp_mm, gp_add = ([sem(f"{n}{k}") for k in range(3)] for n in ("gp_oh", "gp_mm", "gp_add"))
        gp_idx, gp_got, gp_msg = ([sem(f"{n}{k}") for k in range(2)] for n in ("gp_idx", "gp_got", "gp_msg"))
        gp_ea, gp_tr, gp_ev, gp_prod, gp_sum, gp_relu = (sem(n) for n in ("gp_ea", "gp_tr", "gp_ev", "gp_prod", "gp_sum", "gp_relu"))
        gp_step, layer_done = sem("gp_step"), sem("layer_done")
        iota_copied = sem("iota_copied")
        hist_step, sign_step = sem("hist_step"), sem("sign_step")
        block_ready, blocks_ready, over_ready, w0c_ready = (sem(n) for n in ("block_ready", "blocks_ready", "over_ready", "w0c_ready"))
        gp_row, gp_turn = sem("gp_row"), sem("gp_turn")
        gp_step2 = [sem(f"gp_shift{k}") for k in range(2)]

        def wait(eng, s, n):
            if not isinstance(n, int) or n > 0:
                eng.wait_ge(s, n)

        def linker(eng, s):
            count = [0]

            def link(ins):
                count[0] += 1
                ins.then_inc(s, 1)
                eng.wait_ge(s, count[0])
            return link

        def rounds(eng, body):
            body(0, True, False)
            with eng.Fori(1, ROUNDS - 1) as i:
                body(i, False, False)
            body(ROUNDS - 1, False, True)

        def one(i):
            return bass.ds(i, 1) if not isinstance(i, int) else slice(i, i + 1)

        def edge_rows(a):
            return a.rearrange("(r e) -> r e", e=RE)

        EDGE_T = [(a, k, min(GROUP4, TPR - k)) for a in range(3) for k in range(0, TPR, GROUP4)]
        HT_T = NC // GROUP4
        NMG = NC // MG
        PAIRS = -(-NC // (2 * GROUP4))

        def halves(n):
            return min(2, NC // GROUP4 - 2 * n)

        block = ctx.enter_context(nc.Block())

        @block.sync
        def _(sp):
            sp.dma_start(dst_e.bitcast(i32), edge_rows(dst)).then_inc(ld_dst, 16)
            sp.dma_start(xres[:, :, :], x.rearrange("(p c) d -> p c d", c=NC)).then_inc(ld_x, 16)
            sp.dma_start(src_e.bitcast(i32), edge_rows(src)).then_inc(ld_src, 16)
            sp.dma_start(wgt_e, edge_rows(edge_weight)).then_inc(ld_wgt, 16)
            sp.dma_start(w0_s[:, :], w0).then_inc(ld_par, 16)
            sp.dma_start(w1_s[:, :], w1).then_inc(ld_par, 16)
            for n, b in enumerate((b0, b2)):
                sp.dma_start(rows[:, n, :], b.partition_broadcast(NP)).then_inc(ld_par, 16)
            for h in range(2):
                sp.dma_start(b1_c[h * D:(h + 1) * D, :], b1.rearrange("(d o) -> d o", o=1)).then_inc(ld_par, 16)
            for j in range(TILES):
                sp.dma_start(be_row[:, j, :], be.rearrange("(o d) -> o d", o=1)).then_inc(ld_par, 16)
            sp.wait_ge(diag_zeroed, 1)
            for h in range(2):
                sp.dma_start(w2_s[h * D:(h + 1) * D, h, :], w2).then_inc(ld_par, 16)
            for j in range(TILES - 1):
                sp.dma_start(we_s[j * ED:(j + 1) * ED, j, :], we).then_inc(ld_par, 16)
            sp.wait_ge(meta_ready, 1)
            sp.dma_start(meta_dram[0:NSEC].rearrange("(r s) -> r s", s=SECTIONS), meta_i[:, :]).then_inc(meta_stored, 16)
            sp.wait_ge(over_ready, 1)
            sp.dma_start(meta_dram[NSEC:].rearrange("(r o) -> r o", o=1), over[:, :].bitcast(i32)).then_inc(meta_stored, 16)
            sp.wait_ge(meta_stored, 32)
            sp.dma_start(meta_row[:, :], meta_dram.rearrange("(o k) -> o k", o=1)).then_inc(meta_loaded, 16)
            sp.wait_ge(flag_ready, 1)
            far = sp.value_load(flag_i[0:1, 0:1], min_val=0, max_val=1)

            def general_dst(k, after, n):
                sp.wait_ge(after, n)
                for s in range(SECTIONS):
                    sp.dma_start(left_i[:, :, s * TILES:(s + 1) * TILES].bitcast(i32),
                                 dst.rearrange("(r s p j) -> s p r j", s=SECTIONS, p=P, j=TILES)[s]).then_inc(gp_dst, 16)

            with sp.If(far > 0):
                general_dst(0, xc_ready, CH)
            sp.wait_ge(degs_ready, 1)
            sp.dma_start(deg_dram.rearrange("(g h l) -> h g l", g=HG, h=HP), degs[:, :, :]).then_inc(deg_stored, 16)
            sp.wait_ge(deg_stored, 16)
            sp.dma_start(deg[:, :], deg_dram[0:N].rearrange("(p c) -> p c", c=NC)).then_inc(deg_loaded, 16)

            def store_table(L):
                t = table_dram[L].rearrange("(p c) d -> p c d", c=NC)
                for c in range(CH):
                    sp.wait_ge(chunk_ready, L * CH + c + 1)
                    sp.dma_start(t[:, c * CHC:(c + 1) * CHC, :], tbl3[:, c * CHC:(c + 1) * CHC, :]).then_inc(chunk_stored, 16)

            store_table(0)
            with sp.If(far > 0):
                general_dst(1, chunk_stored, 16 * CH)
            store_table(1)

            def load_round(i, first, last):
                for s in range(SECTIONS):
                    if not first:
                        sp.wait_ge(ea_tr, 2 * (i * SECTIONS + s - SECTIONS + 1))
                    sp.dma_start(ea[:, s, :], ea_view[i, s]).then_inc(ea_loaded[s], 16)
            rounds(sp, load_round)
            with sp.If(far > 0):
                general_dst(2, chunk_stored, 32 * CH)
                sp.wait_ge(ea_prod, NSEC)
                with sp.Fori(0, ROUNDS) as i:
                    sp.wait_ge(gp_step, i + 1)
                    sp.dma_start(ea[:, :, :], edge_attr.rearrange("(r s p j) d -> r p s (j d)", s=SECTIONS, p=P, j=TILES)[i]).then_inc(gp_ea, 16)
            o = out.rearrange("(p c) d -> p c d", c=NC)
            for c in range(CH):
                sp.wait_ge(z2_ev, -(-(c + 1) * CHC // (2 * GROUP4)))
                sp.dma_start(o[:, c * CHC:(c + 1) * CHC, :], xres[:, c * CHC:(c + 1) * CHC, :]).then_inc(out_stored, 16)
            sp.wait_ge(out_stored, 16 * CH)

        @block.gpsimd
        def _(pool):
            link = linker(pool, pool_step)
            link(nc.gpsimd.memset(we_s[:, :, :], 0.0))
            nc.gpsimd.memset(w2_s[:, :, :], 0.0).then_inc(diag_zeroed, 1)
            link(nc.gpsimd.iota(iota_g[:, :], pattern=[[1, GEN]], base=0, channel_multiplier=0,
                                allow_small_or_imprecise_dtypes=True))
            link(nc.gpsimd.tensor_scalar(half_off[:, :], iota_g[:, 0:WINDOW + 1], -1.0, 0.5, ALU.mult, ALU.add))
            link(nc.gpsimd.memset(ones[:, :], 1.0))
            link(nc.gpsimd.memset(ident[:, :], 0.0))
            nc.gpsimd.affine_select(out=ident[:, :], in_=ident[:, :], compare_op=ALU.not_equal, fill=1.0, base=0,
                                    pattern=[[-1, P]], channel_multiplier=1).then_inc(consts_ready, 1)
            pool.wait_ge(ld_src, 16)
            nc.gpsimd.tensor_copy(src_e, src_e.bitcast(i32)).then_inc(srcf_ready, 1)
            pool.wait_ge(ld_x, 16)
            half = D // 2
            link(nc.gpsimd.tensor_tensor(tbl3[:, :, 0:half], xres[:, :, 0:half], xres[:, :, half:D], ALU.add))
            while half > 1:
                half //= 2
                link(nc.gpsimd.tensor_tensor(tbl3[:, :, 0:half], tbl3[:, :, 0:half], tbl3[:, :, half:2 * half], ALU.add))
            link(nc.gpsimd.tensor_scalar(mean[:, :], tbl3[:, :, 0:1].rearrange("p c o -> p (c o)"), 1.0 / D, None, ALU.mult))
            for c in range(CH):
                cs = slice(c * CHC, (c + 1) * CHC)
                nc.gpsimd.tensor_tensor(xres[:, cs, :], xres[:, cs, :],
                                        mean[:, cs].unsqueeze(2).to_broadcast([NP, CHC, D]),
                                        ALU.subtract).then_inc(xc_ready, 1)
            pool.wait_ge(block_ready, 1)
            for n in range(LOG_W):
                size = float(WINDOW >> (n + 1))
                link(nc.gpsimd.tensor_scalar(bits[:, n, :], bl[:, :], size, None, ALU.is_ge))
                link(nc.gpsimd.tensor_scalar(bit_step[:, :], bits[:, n, :], size, None, ALU.mult))
                link(nc.gpsimd.tensor_tensor(bl[:, :], bl[:, :], bit_step[:, :], ALU.subtract))
            for s in range(SECTIONS):
                o = ohb_of(s)
                link(nc.gpsimd.memset(o[:, 0:1], 0.0))
                link(nc.gpsimd.tensor_scalar(o[:, 1:HI + 1], iota_g[0:ROUNDS, 0:HI], bh[:, s:s + 1], None, ALU.is_equal))
            pool.sem_inc(blocks_ready, 1)
            pool.wait_ge(edge_ev, len(EDGE_T))
            pool.wait_ge(over_ready, 1)
            pool.wait_ge(rel_ready, 2)
            nc.gpsimd.memset(agg[0:D, :], 0.0).then_inc(agg_zeroed, 1)
            pool.wait_ge(flag_ready, 1)
            far = pool.value_load(flag_i[0:1, 0:1], min_val=0, max_val=1)

            def gather(L, s, j, done):
                nc.gpsimd.indirect_dma_start(
                    out=g[:, s, j, :], out_offset=None, in_=table_dram[L][:, :],
                    in_offset=bass.IndirectOffsetOnAxis(ap=stage[:, s, j:j + 1], axis=0)).then_inc(done, 16)

            for L in range(2):
                pool.wait_ge(chunk_stored, 16 * CH * (L + 1))

                def gather_round(i, first, last):
                    for s in range(SECTIONS):
                        pool.wait_ge(idx_staged, (i + L * ROUNDS) * SECTIONS + s + 1)
                        pool.sem_inc(pool_turn, 1)
                        for j in range(TILES):
                            gather(L, s, j, gathered[s])
                rounds(pool, gather_round)
                with pool.If(far > 0):
                    with pool.Fori(0, ROUNDS) as i:
                        pool.wait_ge(gp_idx[L], i + 1)
                        pool.sem_inc(pool_turn, 1)
                        for k in range(TPR):
                            gather(L, k // TILES, k % TILES, gp_got[L])

        @block.scalar
        def _(act):
            link = linker(act, act_step)
            act.wait_ge(consts_ready, 1)
            act.wait_ge(rel_ready, 2)
            link(nc.scalar.activation(hit_act, rel_b[:, :], ACT.Relu, bias=half_off[0:ROUNDS, WINDOW:WINDOW + 1],
                                      accum_out=over[:, :]))
            act.sem_inc(over_ready, 1)
            for s in range(SECTIONS):
                for w in range(W_ACT, WINDOW + 1):
                    n = s * (WINDOW + 1 - W_ACT) + w - W_ACT
                    wait(act, sign_step, n - 1)
                    nc.scalar.activation(hit_act[:, n % 2 * SEC_E:(n % 2 + 1) * SEC_E], rel_b[:, s * SEC_E:(s + 1) * SEC_E],
                                         ACT.Sign, bias=half_off[0:ROUNDS, w:w + 1],
                                         accum_out=signs[:, s, w - W_ACT:w - W_ACT + 1]).then_inc(sign_step, 1)
            for n, (a, k, m) in enumerate(EDGE_T):
                act.wait_ge(edge_tr, n + 1)
                to = (rel, idx, wgt)[a]
                nc.scalar.copy(to[:, :, k:k + m].rearrange("p r k -> p k r"),
                               ps[:, n % 4, 0:m * ROUNDS].rearrange("p (k r) -> p k r", r=ROUNDS)).then_inc(edge_ev, 1)
            act.wait_ge(w0_tr, 1)
            nc.scalar.copy(w0T[:, 0:D], ps[0:D, 7, 0:D]).then_inc(w0_ev, 1)

            def squares(L):
                def root(c):
                    cs = slice(c * CHC, (c + 1) * CHC)
                    act.wait_ge(var_ready, L * (CH + 1) + c + 1)
                    nc.scalar.activation(rstd[:, cs], rstd[:, cs], ACT.Sqrt).then_inc(sd_ready, 1)

                for c in range(CH):
                    act.wait_ge(xc_ready, L * CH + c + 1)
                    nc.scalar.activation(hbuf[:, c * CHC:(c + 1) * CHC, :], xres[:, c * CHC:(c + 1) * CHC, :],
                                         ACT.Square).then_inc(sq_ready, 1)
                    if L == 1 and c >= 1:
                        root(c - 1)
                for c in range(CH if L == 0 else 0):
                    root(c)
                if L == 1:
                    root(CH - 1)
            squares(0)
            act.wait_ge(flag_ready, 1)
            far = act.value_load(flag_i[0:1, 0:1], min_val=0, max_val=1)
            def stage_section(i, s):
                nc.scalar.copy(stage[:, s:s + 1, :], idx[:, one(i), s * TILES:(s + 1) * TILES]).then_inc(idx_staged, 1)
                nc.scalar.copy(cols[:, s:s + 1, :, :], relw[:, one(i), :, s * TILES:(s + 1) * TILES]).then_inc(cols_staged, 1)

            act.wait_ge(edge_ev, len(EDGE_T))
            for s in range(SECTIONS):
                stage_section(0, s)
            act.wait_ge(var_ready, CH + 1)
            nc.scalar.activation(norm[:, :], norm[:, :], ACT.Sqrt).then_inc(sd_ready, 1)
            def stage_round(i, first, last):
                if not last:
                    for s in range(SECTIONS):
                        act.wait_ge(agg_done, i * SECTIONS + s + 1)
                        act.sem_inc(act_turn, 1)
                        stage_section(i + 1, s)
            rounds(act, stage_round)
            act.wait_ge(chunk_stored, 16 * CH)
            squares(1)
            aggc = agg[0:D, 0:N].rearrange("f (p c) -> f c p", c=NC)
            for n in range(HT_T):
                act.wait_ge(ht_mm, n + 1)
                nc.scalar.copy(aggc[:, n * GROUP4:(n + 1) * GROUP4, :],
                               ps[0:D, n % 4, 0:GROUP4 * NP].rearrange("f (c p) -> f c p", p=NP)).then_inc(ht_ev, 1)

            def evacuate(q, s, trd, evd, slot):
                t = tr_bank(s)
                act.wait_ge(trd, 2 * q + 2)
                nc.scalar.copy(eaT[:, slot, 0, :], t[:, 0:P]).then_inc(evd, 1)
                nc.scalar.copy(eaT[0:ED, slot, 1, :], t[0:ED, P:2 * P]).then_inc(evd, 1)

            act.wait_ge(layer_done, 1)
            for s in range(SECTIONS):
                stage_section(0, s)
            evacuate(0, 0, ea_tr, ea_ev, 0)

            def act_round(i, first, last):
                for s in range(SECTIONS):
                    q = i * SECTIONS + s
                    if not (last and s == SECTIONS - 1):
                        act.wait_ge(ea_prod, q + 1)
                        evacuate(q + 1, (s + 1) % SECTIONS, ea_tr, ea_ev, ((s + 1) % SECTIONS) % 2)
                    act.wait_ge(summed, q + 1)
                    nc.scalar.activation(msg[:, s, :, :], msg[:, s, :, :], ACT.Relu).then_inc(relued, 1)
                    if not last:
                        stage_section(i + 1, s)
            rounds(act, act_round)
            with act.If(far > 0):
                with act.Fori(0, ROUNDS) as i:
                    for s in range(SECTIONS):
                        q = i * SECTIONS + s
                        evacuate(q, s, gp_tr, gp_ev, s % 2)
                        act.wait_ge(gp_sum, q + 1)
                        nc.scalar.activation(msg[:, s, :, :], msg[:, s, :, :], ACT.Relu).then_inc(gp_relu, 1)
            for n in range(PAIRS):
                act.wait_ge(z1_mm, n + 1)
                if n >= 1:
                    act.wait_ge(z2_mm, n)
                h = D * halves(n)
                nc.scalar.activation(r1[0:h, 0:GROUP4 * NP], ps[0:h, n % 2, 0:GROUP4 * NP], ACT.Relu,
                                     bias=b1_c[0:h, 0:1]).then_inc(z1_ev, 1)

        @block.vector
        def _(dve):
            link = linker(dve, dve_step)

            def mul(o, a, b, op=ALU.mult):
                return nc.vector.tensor_tensor(o, a, b, op)

            dve.wait_ge(ld_dst, 16)
            ds3 = dst_e.bitcast(i32).rearrange("r (s e) -> r s e", s=SECTIONS)
            rel3 = rel_e.rearrange("r (s e) -> r s e", s=SECTIONS)
            link(nc.vector.tensor_reduce(lo[:, :], ds3, AX.X, ALU.min))
            mul(rel3, ds3, lo[:, :].unsqueeze(2).to_broadcast([ROUNDS, SECTIONS, SEC_E]), ALU.subtract).then_inc(rel_ready, 1)
            nc.vector.tensor_copy(meta_i[:, :], lo[:, :]).then_inc(meta_ready, 1)
            dve.wait_ge(rel_ready, 1)
            nc.vector.tensor_copy(rel_b[:, :], rel_e).then_inc(rel_ready, 1)
            dve.wait_ge(meta_ready, 1)
            link(nc.vector.tensor_scalar(block_i[:, :], meta_i[:, :], LOG_W, None, ALU.arith_shift_right))
            link(nc.vector.tensor_copy(bh[:, :], block_i[:, :]))
            nc.vector.scalar_tensor_tensor(bl[:, :], bh[:, :], -float(WINDOW), lo[:, :], ALU.mult, ALU.add).then_inc(block_ready, 1)

            def variance(L, c):
                cs = slice(c * CHC, (c + 1) * CHC)
                dve.wait_ge(sq_ready, L * CH + c + 1)
                link(nc.vector.tensor_reduce(rstd[:, cs], hbuf[:, cs, :], AX.X, ALU.add))
                nc.vector.tensor_scalar(rstd[:, cs], rstd[:, cs], 1.0 / D, EPS, ALU.mult, ALU.add).then_inc(var_ready, 1)

            link(nc.vector.memset(hist[:, :, :], 0.0))
            dve.wait_ge(rel_ready, 2)
            for s in range(SECTIONS):
                for w in range(W_ACT):
                    n = s * W_ACT + w
                    wait(dve, hist_step, n - 1)
                    nc.vector.tensor_scalar(hit[:, n % 2, :], rel_b[:, s * SEC_E:(s + 1) * SEC_E], float(w), 0.0,
                                            ALU.is_equal, ALU.add,
                                            accum_out=hist[:, s, PAD + w:PAD + w + 1]).then_inc(hist_step, 1)
            dve.wait_ge(sign_step, SECTIONS * (WINDOW + 1 - W_ACT))
            dve.wait_ge(hist_step, SECTIONS * W_ACT)
            n = WINDOW - W_ACT
            link(mul(signs[:, :, 0:n], signs[:, :, 0:n], signs[:, :, 1:n + 1], ALU.subtract))
            link(nc.vector.tensor_scalar(hist[:, :, PAD + W_ACT:PAD + WINDOW], signs[:, :, 0:n], 0.5, None, ALU.mult))
            dve.wait_ge(blocks_ready, 1)
            for n in range(LOG_W):
                sh = WINDOW >> (n + 1)
                h0 = hist[:, :, PAD:PAD + 2 * WINDOW]
                link(mul(histd[:, :, :], hist[:, :, PAD - sh:PAD - sh + 2 * WINDOW], h0, ALU.subtract))
                link(mul(histd[:, :, :], histd[:, :, :],
                         bits[:, n, :].unsqueeze(2).to_broadcast([ROUNDS, SECTIONS, 2 * WINDOW])))
                link(mul(h0, h0, histd[:, :, :], ALU.add))
            dve.sem_inc(hist_ready, 1)
            dve.wait_ge(meta_loaded, 16)
            link(nc.vector.tensor_reduce(flag_f[:, :], meta_row[:, NSEC:], AX.X, ALU.max))
            link(nc.vector.tensor_scalar(flag_f[:, :], flag_f[:, :], 0.0, None, ALU.is_gt))
            nc.vector.tensor_copy(flag_i[:, :], flag_f[:, :]).then_inc(flag_ready, 1)
            for c in range(CH // 2):
                variance(0, c)
            dve.wait_ge(degmm_done, 1)
            link(nc.vector.tensor_copy(degs[:, :, :].rearrange("h g l -> h (g l)"), ps[0:HP, 6, 0:HG * WINDOW]))
            far = dve.value_load(flag_i[0:1, 0:1], min_val=0, max_val=1)

            def far_edges(k):
                dve.wait_ge(gp_dst, 16 * SECTIONS * (k + 1))
                nc.vector.tensor_copy(left, left_i.bitcast(i32)).then_inc(gp_ready[k], 1)
                dve.wait_ge(gp_ready[k], 1)
                nc.vector.tensor_scalar(left, left, FAR, None, ALU.subtract).then_inc(gp_ready[k], 1)
                nc.vector.tensor_scalar(left_i, rel[:, :, :], float(WINDOW), None, ALU.is_ge).then_inc(gp_ready[k], 1)
                dve.wait_ge(gp_ready[k], 3)
                mul(left, left, left_i).then_inc(gp_ready[k], 1)
                dve.wait_ge(gp_ready[k], 4)
                nc.vector.tensor_scalar(left, left, FAR, None, ALU.add).then_inc(gp_ready[k], 1)
                dve.wait_ge(gp_ready[k], 5)

            with dve.If(far > 0):
                far_edges(0)
                nc.vector.tensor_copy(left_i.bitcast(i32), left).then_inc(gp_ready[0], 1)
                dve.wait_ge(gp_ready[0], 6)
                nc.vector.tensor_scalar(left_i.bitcast(i32), left_i.bitcast(i32), LOG_W, None,
                                        ALU.arith_shift_right).then_inc(gp_ready[0], 1)
                dve.wait_ge(gp_ready[0], 7)
                nc.vector.tensor_copy(left_i, left_i.bitcast(i32)).then_inc(gp_ready[0], 1)
                dve.wait_ge(gp_ready[0], 8)
                nc.vector.scalar_tensor_tensor(left, left_i, -float(WINDOW), left, ALU.mult, ALU.add).then_inc(gp_ready[0], 1)
                dve.wait_ge(gp_ready[0], 9)
                with dve.Fori(0, ROUNDS) as i:
                    nc.vector.tensor_copy(shift[:, :], left_i[:, bass.ds(i, 1), :].rearrange("p o k -> p (o k)")).then_inc(gp_row, 1)
                    nc.vector.tensor_copy(shift_lo[:, :], left[:, bass.ds(i, 1), :].rearrange("p o k -> p (o k)")).then_inc(gp_row, 1)
                    dve.wait_ge(gp_row, 2 * (i + 1))
                    for k in range(TPR):
                        n = i * TPR + k
                        nc.vector.tensor_scalar(wide[:, 0:HI], iota_g[:, 0:HI], shift[:, k:k + 1], None,
                                                ALU.is_equal).then_inc(gp_oh[0], 1)
                        nc.vector.tensor_scalar(oh[:, 0, 0, :], iota_g[:, 0:WINDOW], shift_lo[:, k:k + 1], None,
                                                ALU.is_equal).then_inc(gp_oh[0], 1)
                        dve.wait_ge(gp_mm[0], n + 1)
                        mul(degs[:, :, :].rearrange("h g l -> h (g l)"), degs[:, :, :].rearrange("h g l -> h (g l)"),
                            ps[0:HP, 4, 0:HG * WINDOW], ALU.add).then_inc(gp_add[0], 1)
                        dve.wait_ge(gp_add[0], n + 1)
            dve.sem_inc(degs_ready, 1)
            for c in range(CH // 2, CH):
                variance(0, c)
            dve.wait_ge(ld_par, 16 * LOADS)
            link(nc.vector.tensor_reduce(b0_mean[:, :], rows[:, 0, :], AX.X, ALU.add))
            link(nc.vector.tensor_scalar(b0_mean[:, :], b0_mean[:, :], 1.0 / D, None, ALU.mult))
            link(nc.vector.tensor_scalar(rows[:, 0, :], rows[:, 0, :], b0_mean[:, 0:1], None, ALU.subtract))
            link(nc.vector.tensor_scalar(mean[:, :], mean[:, :], b0_mean[:, 0:1], None, ALU.add))
            dve.wait_ge(w0_ev, 1)
            link(nc.vector.tensor_reduce(w0T[:, D:D + 1], w0T[:, 0:D], AX.X, ALU.add))
            link(nc.vector.tensor_scalar(w0T[:, D:D + 1], w0T[:, D:D + 1], 1.0 / D, None, ALU.mult))
            nc.vector.tensor_scalar(w0T[:, 0:D], w0T[:, 0:D], w0T[:, D:D + 1], None, ALU.subtract).then_inc(w0c_ready, 1)
            dve.wait_ge(sd_ready, CH)
            link(nc.vector.reciprocal(rstd[:, :], rstd[:, :]))
            dve.wait_ge(deg_loaded, 16)
            nc.vector.tensor_scalar(norm[:, :], deg[:, :], 1.0, None, ALU.max).then_inc(var_ready, 1)
            dve.wait_ge(sd_ready, CH + 1)
            link(nc.vector.reciprocal(norm[:, :], norm[:, :]))
            link(nc.vector.tensor_scalar(deg[:, :], deg[:, :], 0.0, None, ALU.is_gt))
            link(mul(norm[:, :], norm[:, :], deg[:, :]))
            link(mul(rstd[:, :], rstd[:, :], norm[:, :]))

            def normed_rows(c):
                cs = slice(c * CHC, (c + 1) * CHC)
                nc.vector.scalar_tensor_tensor(tbl3[:, cs, :], xres[:, cs, :], 0.0,
                                               rstd[:, cs].unsqueeze(2).to_broadcast([NP, CHC, D]),
                                               ALU.max, ALU.mult).then_inc(chunk_ready, 1)
            for c in range(CH):
                normed_rows(c)
            nc.vector.tensor_copy(iota_p, iota_g[:, 0:WINDOW]).then_inc(iota_copied, 1)
            dve.wait_ge(iota_copied, 1)
            dve.wait_ge(agg_zeroed, 1)

            def layer(L):
                if L == 0:
                    dve.wait_ge(chunk_ready, CH)
                    link(mul(xres[:, :, :], xres[:, :, :], rows[:, 0, :].unsqueeze(1).to_broadcast([NP, NC, D]), ALU.add))
                else:
                    dve.wait_ge(chunk_ready, 2 * CH)
                    link(mul(xres[:, :, :], xres[:, :, :], mean[:, :].unsqueeze(2).to_broadcast([NP, NC, D]), ALU.add))
                    link(mul(xres[:, :, :], xres[:, :, :], rows[:, 1, :].unsqueeze(1).to_broadcast([NP, NC, D]), ALU.add))
                    dve.wait_ge(ht_ev, HT_T)

                def dve_round(i, first, last):
                    for s in range(SECTIONS):
                        q = i * SECTIONS + s
                        Q = q + L * NSEC
                        base = dve.value_load(meta_row[0:1, one(q)],
                                              min_val=0, max_val=N - 1)
                        dve.wait_ge(cols_staged, Q + 1)
                        for j in range(TILES):
                            lastoh = nc.vector.tensor_scalar(oh[:, s, j, :], iota_p, cols[:, s, 0, j:j + 1],
                                                             cols[:, s, 1, j:j + 1] if L == 0 else None,
                                                             ALU.is_equal, *([ALU.mult] if L == 0 else []))
                        lastoh.then_inc(onehot_ready, 1)
                        if L == 1:
                            dve.wait_ge(gathered[s], (i + ROUNDS + 1) * 16 * TILES)
                            dve.wait_ge(ea_prod, q + 1)
                            mul(msg[:, s, :, :], mbank(s).rearrange("p (j d) -> p j d", d=D), g[:, s, :, :],
                                ALU.add).then_inc(summed, 1)
                        dve.wait_ge(agg_done, Q + 1)
                        wait(dve, added, Q)
                        a = agg[0:D, bass.ds(base, WINDOW)]
                        mul(a, a, win(s), ALU.add).then_inc(added, 1)
                rounds(dve, dve_round)
                dve.wait_ge(added, NSEC * (L + 1))
                with dve.If(far > 0):
                    far_edges(L + 1)
                    with dve.Fori(0, ROUNDS) as i:
                        nc.vector.tensor_copy(shift[:, :], left[:, bass.ds(i, 1), :].rearrange("p o k -> p (o k)")).then_inc(gp_step2[L], 1)
                        nc.vector.tensor_copy(stage[:, :, :].rearrange("p s j -> p (s j)"),
                                              idx[:, bass.ds(i, 1), :].rearrange("p o k -> p (o k)")).then_inc(gp_idx[L], 1)
                        dve.wait_ge(gp_got[L], (i + 1) * 16 * TPR)
                        if L == 0:
                            mul(msg[:, :, :, :].rearrange("p s j d -> p (s j) d"), g[:, :, :, :].rearrange("p s j d -> p (s j) d"),
                                wgt[:, bass.ds(i, 1), :].rearrange("p o k -> p (o k)").unsqueeze(2).to_broadcast([P, TPR, D])
                                ).then_inc(gp_msg[0], 1)
                        else:
                            for s in range(SECTIONS):
                                dve.wait_ge(gp_prod, i * SECTIONS + s + 1)
                                mul(msg[:, s, :, :], mbank(s).rearrange("p (j d) -> p j d", d=D), g[:, s, :, :],
                                    ALU.add).then_inc(gp_sum, 1)
                        with dve.Fori(0, NGEN) as v:
                            for k in range(TPR):
                                n = (i * NGEN + v) * TPR + k
                                if k == 0:
                                    dve.wait_ge(gp_step2[L], i * (NGEN + 1) + v + 1)
                                nc.vector.tensor_scalar(wide[:, :], iota_g[:, :], shift[:, k:k + 1], None,
                                                        ALU.is_equal).then_inc(gp_oh[L + 1], 1)
                                dve.wait_ge(gp_mm[L + 1], n + 1)
                            nc.vector.tensor_scalar(shift[:, :], shift[:, :], float(GEN), None, ALU.subtract).then_inc(gp_step2[L], 1)
                            a = agg[0:D, bass.ds(v * GEN, GEN)]
                            mul(a, a, ps[0:D, 7, 0:GEN], ALU.add).then_inc(gp_add[L + 1], 1)
                            dve.wait_ge(gp_add[L + 1], i * NGEN + v + 1)
                dve.sem_inc(layer_done, 1)

            layer(0)
            def finish(c):
                cs = slice(c * CHC, (c + 1) * CHC)
                dve.wait_ge(sd_ready, CH + 1 + c + 1)
                link(nc.vector.reciprocal(rstd[:, cs], rstd[:, cs]))
                normed_rows(c)

            for n in range(NMG):
                cs = slice(n * MG, (n + 1) * MG)
                p = ps[0:NP, n % 4, 0:MG * (D + 1)].rearrange("p (c d) -> p c d", d=D + 1)
                c = (n + 1) * MG // CHC - 1
                dve.wait_ge(mid_mm, n + 1)
                mul(scratch[:, n % 2, :, :], p, norm[:, cs].unsqueeze(2).to_broadcast([NP, MG, D + 1])).then_inc(mid_ev, 1)
                dve.wait_ge(mid_ev, n + 1)
                mul(mean[:, cs], mean[:, cs], scratch[:, n % 2, :, D:D + 1].rearrange("p c o -> p (c o)"), ALU.add)
                last = mul(xres[:, cs, :], xres[:, cs, :], scratch[:, n % 2, :, 0:D], ALU.add)
                if (n + 1) * MG % CHC == 0:
                    last.then_inc(xc_ready, 1)
                    if c >= 1:
                        variance(1, c - 1)
                    if c >= 2:
                        finish(c - 2)
            finish(CH - 2)
            variance(1, CH - 1)
            finish(CH - 1)
            layer(1)
            for n in range(PAIRS):
                h = halves(n)
                cs = slice(2 * n * GROUP4, (2 * n + h) * GROUP4)
                a = xres[:, cs, :].rearrange("p (h c) d -> p h c d", h=h)
                dve.wait_ge(z2_mm, n + 1)
                mul(a, a, ps[0:NP, 2 + n % 2, 0:GROUP4 * h * D].rearrange("p (c h d) -> p h c d", h=h, d=D),
                    ALU.add).then_inc(z2_ev, 1)

        @block.tensor
        def _(pe):
            pe.wait_ge(consts_ready, 1)
            pe.wait_ge(ld_par, 16 * LOADS)
            nc.tensor.transpose(ps[0:D, 7, 0:D], w0_s[:, :], ident[0:D, 0:D]).then_inc(w0_tr, 1)
            for n, (a, k, m) in enumerate(EDGE_T):
                if k == 0:
                    if a == 0:
                        pe.wait_ge(rel_ready, 2)
                    elif a == 1:
                        pe.wait_ge(srcf_ready, 1)
                    else:
                        pe.wait_ge(ld_wgt, 16)
                if n >= 4:
                    pe.wait_ge(edge_ev, n - 3)
                arr = (rel_e, src_e, wgt_e)[a].rearrange("r (s p j) -> r s j p", s=SECTIONS, p=P)
                for t in range(m):
                    last = nc.tensor.transpose(ps[:, n % 4, t * ROUNDS:(t + 1) * ROUNDS],
                                               arr[:, (k + t) // TILES, (k + t) % TILES, :], ident[0:ROUNDS, 0:ROUNDS])
                last.then_inc(edge_tr, 1)
            pe.wait_ge(blocks_ready, 1)
            pe.wait_ge(hist_ready, 1)
            for gp in range(HG):
                steps = [(s, half) for s in range(SECTIONS) for half in range(2)]
                for n, (s, half) in enumerate(steps):
                    o = ohb_of(s)
                    last = nc.tensor.matmul(ps[0:HP, 6, gp * WINDOW:(gp + 1) * WINDOW],
                                            o[:, 1 - half + gp * HP:1 - half + (gp + 1) * HP],
                                            hist[:, s, PAD + half * WINDOW:PAD + (half + 1) * WINDOW],
                                            start=(n == 0), stop=(n == len(steps) - 1))
            last.then_inc(degmm_done, 1)
            pe.wait_ge(flag_ready, 1)
            far = pe.value_load(flag_i[0:1, 0:1], min_val=0, max_val=1)
            with pe.If(far > 0):
                with pe.Fori(0, ROUNDS) as i:
                    for k in range(TPR):
                        pe.wait_ge(gp_oh[0], 2 * (i * TPR + k + 1))
                        for gp in range(HG):
                            last = nc.tensor.matmul(ps[0:HP, 4, gp * WINDOW:(gp + 1) * WINDOW],
                                                    wide[:, gp * HP:(gp + 1) * HP], oh[:, 0, 0, :], start=True, stop=True)
                        last.then_inc(gp_mm[0], 1)

            def transposes(s, done):
                t = tr_bank(s)
                cut = (TILES - 1) * ED
                nc.tensor.transpose(t[:, 0:P], ea[:, s, 0:cut], ident[:, :]).then_inc(done, 1)
                nc.tensor.transpose(t[0:ED, P:2 * P], ea[:, s, cut:cut + ED], ident[:, :]).then_inc(done, 1)
                nc.tensor.matmul(mbank(s), ones[:, :], be_row[:, :, :].rearrange("o j d -> o (j d)"), start=True, stop=False)

            def products(s, done):
                nc.tensor.matmul(mbank(s)[:, 0:(TILES - 1) * D], eaT[:, s % 2, 0, :],
                                 we_s[:, :, :].rearrange("p j d -> p (j d)"), start=False, stop=False)
                last = nc.tensor.matmul(mbank(s)[:, (TILES - 1) * D:], eaT[0:ED, s % 2, 1, :], we_s[0:ED, 0, :],
                                        start=False, stop=True)
                last.then_inc(done, 1)

            def window_sums(rows_of, s):
                for j in range(TILES):
                    last = nc.tensor.matmul(win(s), rows_of[:, s, j, :], oh[:, s, j, :], start=(j == 0), stop=(j == TILES - 1))
                last.then_inc(agg_done, 1)

            def attributes(q, s, i):
                pe.wait_ge(ea_loaded[s], 16 * (i + 1))
                transposes(s, ea_tr)
                pe.wait_ge(ea_ev, 2 * (q + 1))
                products(s, ea_prod)

            for L in range(2):
                if L == 1:
                    attributes(0, 0, 0)

                def pe_round(i, first, last):
                    for s in range(SECTIONS):
                        q = i * SECTIONS + s
                        if L == 1 and not (last and s == SECTIONS - 1):
                            attributes(q + 1, (s + 1) % SECTIONS, i + (1 if s == SECTIONS - 1 else 0))
                        pe.wait_ge(onehot_ready, q + L * NSEC + 1)
                        if L == 0:
                            pe.wait_ge(gathered[s], (i + 1) * 16 * TILES)
                            window_sums(g, s)
                        else:
                            pe.wait_ge(relued, q + 1)
                            window_sums(msg, s)
                rounds(pe, pe_round)
                with pe.If(far > 0):
                    with pe.Fori(0, ROUNDS) as i:
                        if L == 0:
                            pe.wait_ge(gp_msg[0], i + 1)
                        else:
                            pe.sem_inc(gp_step, 1)
                            pe.wait_ge(gp_ea, 16 * (i + 1))
                            for s in range(SECTIONS):
                                transposes(s, gp_tr)
                                pe.wait_ge(gp_ev, 2 * (i * SECTIONS + s + 1))
                                products(s, gp_prod)
                                pe.wait_ge(gp_relu, i * SECTIONS + s + 1)
                        pe.sem_inc(gp_turn, 1)
                        with pe.Fori(0, NGEN) as v:
                            for k in range(TPR):
                                pe.wait_ge(gp_oh[L + 1], (i * NGEN + v) * TPR + k + 1)
                                nc.tensor.matmul(ps[0:D, 7, 0:GEN], msg[:, k // TILES, k % TILES, :], wide[:, :],
                                                 start=(k == 0), stop=(k == TPR - 1)).then_inc(gp_mm[L + 1], 1)
                pe.wait_ge(layer_done, L + 1)
                aggc = agg[0:D, 0:N].rearrange("f (p c) -> f c p", c=NC)
                if L == 0:
                    pe.wait_ge(w0c_ready, 1)
                    for n in range(NMG):
                        if n >= 4:
                            pe.wait_ge(mid_ev, n - 3)
                        for c in range(MG):
                            last = nc.tensor.matmul(ps[0:NP, n % 4, c * (D + 1):(c + 1) * (D + 1)],
                                                    aggc[:, n * MG + c, :], w0T[:, :], start=True, stop=True)
                        last.then_inc(mid_mm, 1)
                    pe.wait_ge(chunk_ready, 2 * CH)
                    for n in range(HT_T):
                        if n >= 4:
                            pe.wait_ge(ht_ev, n - 3)
                        for c in range(GROUP4):
                            last = nc.tensor.transpose(ps[0:D, n % 4, c * NP:(c + 1) * NP], tbl3[:, n * GROUP4 + c, :],
                                                       ident[0:NP, 0:NP])
                        last.then_inc(ht_mm, 1)
                    pe.wait_ge(ht_ev, HT_T)
                else:
                    def first_product(n):
                        if n >= 2:
                            pe.wait_ge(z1_ev, n - 1)
                        for h in range(halves(n)):
                            k = (2 * n + h) * GROUP4
                            last = nc.tensor.matmul(ps[h * D:(h + 1) * D, n % 2, 0:GROUP4 * NP], w1_s[:, :],
                                                    aggc[:, k:k + GROUP4, :], start=True, stop=True)
                        last.then_inc(z1_mm, 1)
                    first_product(0)
                    for n in range(PAIRS):
                        if n + 1 < PAIRS:
                            first_product(n + 1)
                        pe.wait_ge(z1_ev, n + 1)
                        if n >= 2:
                            pe.wait_ge(z2_ev, n - 1)
                        h = halves(n) * D
                        for c in range(GROUP4):
                            last = nc.tensor.matmul(ps[0:NP, 2 + n % 2, c * h:(c + 1) * h], r1[0:h, c * NP:(c + 1) * NP],
                                                    w2_s[0:h, :, :].rearrange("p h d -> p (h d)")[:, 0:h],
                                                    start=True, stop=True)
                        last.then_inc(z2_mm, 1)


_INS = ['x', 'src', 'dst', 'edge_attr_32', 'edge_weight', 'L0_gnn_weight', 'L0_gnn_b', 'L1_gnn_We', 'L1_gnn_be',
        'L1_gnn_W1', 'L1_gnn_b1', 'L1_gnn_W2', 'L1_gnn_b2']


def kernel(**inputs):
    import numpy as _np
    import concourse.bacc as _bacc
    from concourse import mybir as _mybir
    from concourse.bass_utils import run_bass_kernel_spmd as _run

    nc = _bacc.Bacc("TRN2", target_bir_lowering=False, num_devices=1)
    arrays, args = {}, []
    for name in _INS:
        a = _np.ascontiguousarray(inputs[name])
        arrays[f"in_{name}_dram"] = a
        args.append(nc.dram_tensor(f"in_{name}_dram", a.shape, _mybir.dt.from_np(a.dtype), kind="ExternalInput").ap())
    out = nc.dram_tensor("out_0_dram", inputs['x'].shape, _mybir.dt.float32, kind="ExternalOutput").ap()
    gnn_preln_two_layers(nc, *args, out)
    r = _run(nc, [arrays], core_ids=[0])
    return r.results[0]["out_0_dram"]
```

```python
import concourse.bass as bass
from concourse import mybir
from contextlib import ExitStack


def gnn_preln_two_layers(nc, x, src, dst, edge_attr, edge_weight, w0, b0, we, be, w1, b1, w2, b2, out):
    fp32, fp16, bf16, i32 = mybir.dt.float32, mybir.dt.float16, mybir.dt.bfloat16, mybir.dt.int32
    ALU = mybir.AluOpType
    ACT = mybir.ActivationFunctionType
    AX = mybir.AxisListType

    N, D = x.shape
    E, ED = edge_attr.shape
    P = 128
    NP = 125
    NC = N // NP
    TILES, SECTIONS = 5, 5
    LOG_W = 5
    WINDOW = 2 ** LOG_W
    TPR = TILES * SECTIONS
    SEC_E = TILES * P
    ROUNDS = E // (TPR * P)
    RE = TPR * P
    NSEC = ROUNDS * SECTIONS
    HI = 392
    HG, HP = 4, 98
    GEN = 500
    NGEN = N // GEN
    FAR = 20000.0
    CH, CHC = 10, NC // 10
    PARTS = 3
    LAST = SECTIONS - 1
    LOG_Q = 2
    QUAD = 2 ** LOG_Q
    NG = NC // QUAD
    STEPS = (0, 7, 13, 19, NG)
    LOOKS = len(STEPS) - 1
    EPS = 1e-5
    EARLY = 3
    MG = 5
    LOADS = 2 + 3 + 2 + 2 + TILES - 1
    GROUP4 = 4
    W_ACT = 23
    assert NP * NC == N and ROUNDS * RE == E and ROUNDS <= P and NGEN * GEN == N and HP * HG * WINDOW >= N
    assert NG * QUAD == NC and NG * P <= NC * D and LOOKS == LAST

    meta_dram = nc.dram_tensor("section_meta", (NSEC + ROUNDS,), i32, kind="Internal").ap()
    deg_dram = nc.dram_tensor("degrees", (HG * HP * WINDOW,), fp32, kind="Internal").ap()
    table_dram = [nc.dram_tensor(f"table{L}", (N, D), fp32, kind="Internal").ap() for L in range(2)]

    ea_view = edge_attr.rearrange("(r s p j) d -> r s p (j d)", s=SECTIONS, p=P, j=TILES)
    ctx = ExitStack()
    with ctx:
        def sb(name, shape, dt=fp32):
            return ctx.enter_context(nc.sbuf_tensor(name, shape, dt))

        def sem(name):
            return ctx.enter_context(nc.semaphore(name))

        agg = sb("agg", [P, 4 * RE])
        dst_e = agg[0:ROUNDS, 0:RE]
        src_e = agg[0:ROUNDS, RE:2 * RE]
        wgt_e = agg[0:ROUNDS, 2 * RE:3 * RE]
        rel_e = agg[0:ROUNDS, 3 * RE:4 * RE]
        rel_b = sb("rel_b", [ROUNDS, RE], bf16)
        xres = sb("xres", [NP, NC, D])
        node_space = sb("node_space", [P, 2 * NC * D])
        hbuf = node_space[0:NP, 0:NC * D].rearrange("p (c d) -> p c d", d=D)
        tbl = node_space[:, NC * D:]
        planes = node_space[0:NP, :].bitcast(bf16).rearrange("p (t c d) -> p t c d", t=PARTS + 1, d=D)
        hot = node_space[0:NP, :].bitcast(bf16)[:, PARTS * NC * D:PARTS * NC * D + NG * P].rearrange(
            "p (g e) -> p g e", e=P)
        tbl3 = tbl[0:NP, :].rearrange("p (c d) -> p c d", d=D)
        left = tbl[:, 0:ROUNDS * TPR].rearrange("p (r k) -> p r k", k=TPR)
        left_i = tbl[:, ROUNDS * TPR:2 * ROUNDS * TPR].rearrange("p (r k) -> p r k", k=TPR)
        idx = sb("idx", [P, ROUNDS, TPR])
        relw = sb("relw", [P, ROUNDS, 2, TPR])
        rel, wgt = relw[:, :, 0, :], relw[:, :, 1, :]
        stage = sb("stage", [P, SECTIONS, TILES], i32)
        cols = sb("cols", [P, SECTIONS, 2, TILES])
        g = sb("g", [P, SECTIONS, TILES, D])
        msg = sb("msg", [P, SECTIONS, TILES, D])
        oh = sb("oh", [P, SECTIONS, TILES, WINDOW])
        ea = sb("ea", [P, SECTIONS, TILES * ED])
        eaT = sb("eaT", [P, 2, 2, P])
        iota_g = sb("iota_g", [P, GEN])
        wide = sb("wide", [P, GEN])
        shift = sb("shift", [P, TPR])
        shift_lo = sb("shift_lo", [P, TPR])
        ident = sb("ident", [P, P])
        group_id = sb("group_id", [NP, NG])
        group = sb("group", [P, ROUNDS])
        place = sb("place", [P, ROUNDS, QUAD])
        id_col = sb("id_col", [P, 1])
        quad = sb("quad", [P, QUAD, D])
        shifted, offset = wide[:, 0:ROUNDS], wide[:, ROUNDS:2 * ROUNDS]
        meta_row = sb("meta_row", [1, NSEC + ROUNDS], i32)
        flag_f = sb("flag_f", [1, 1])
        flag_i = sb("flag_i", [1, 1], i32)
        lo = sb("lo", [ROUNDS, SECTIONS])
        meta_i = sb("meta_i", [ROUNDS, SECTIONS], i32)
        over = sb("over", [ROUNDS, 1])
        block_i = sb("block_i", [ROUNDS, SECTIONS], i32)
        bl = sb("bl", [ROUNDS, SECTIONS])
        bh = sb("bh", [ROUNDS, SECTIONS])
        bits = sb("bits", [ROUNDS, LOG_W, SECTIONS])
        bit_step = sb("bit_step", [ROUNDS, SECTIONS])
        PAD = WINDOW // 2
        assert SEC_E <= 2048
        hist = sb("hist", [ROUNDS, SECTIONS, PAD + 2 * WINDOW], fp16)
        histd = sb("histd", [ROUNDS, SECTIONS, 2 * WINDOW], fp16)
        signs = sb("signs", [ROUNDS, SECTIONS, WINDOW + 1 - W_ACT])
        half_off = sb("half_off", [P, WINDOW + 1])
        flat_msg = msg[0:ROUNDS, :, :, :].rearrange("p s j d -> p (s j d)").bitcast(fp16)
        hit = ea[0:ROUNDS, 0:4, :].rearrange("p s d -> p (s d)").bitcast(bf16).rearrange("p (h e) -> p h e", h=2)
        hit_act = g[0:ROUNDS, :, :, :].rearrange("p s j d -> p (s j d)").bitcast(bf16)[:, 0:RE]

        def ohb_of(s):
            return flat_msg[:, s * (HI + 2):s * (HI + 2) + HI + 1]

        degs = sb("degs", [HP, HG, WINDOW])
        scratch = msg[0:NP, :, :, :].rearrange("p s j d -> p (s j d)")[:, 0:2 * MG * (D + 1)].rearrange(
            "p (n c d) -> p n c d", n=2, c=MG)
        deg = sb("deg", [NP, NC])
        norm = sb("norm", [NP, NC])
        mean = sb("mean", [NP, NC])
        rstd = sb("rstd", [NP, NC])
        w0_s = sb("w0_s", [D, D])
        w0T = sb("w0T", [D, D + 1])
        w1_s = sb("w1_s", [D, D])
        w2_s = sb("w2_s", [2 * D, 2, D])
        we_s = sb("we_s", [P, TILES - 1, D])
        rows = sb("rows", [NP, 3, D])
        b0_mean = sb("b0_mean", [NP, 1])
        b1_c = sb("b1_c", [2 * D, 1])

        r1 = eaT[:, :, :, :].rearrange("p a b c -> p (a b c)")
        ps = ctx.enter_context(nc.psum_tensor("ps", [P, 8, 512], fp32))

        tr_bank = ps[:, 0, :]

        def mbank(s):
            return ps[:, 2 + s % 3, 0:TILES * D]

        def win(s):
            return ps[0:D, 7, s * WINDOW:(s + 1) * WINDOW]

        iota_p = ps[:, 5, 0:WINDOW]

        ids_p = ps[0:NP, 5, P:2 * P]
        rows_p = [ps[:, bank, 0:PARTS * QUAD // 2 * D] for bank in (6, 1)]

        ld_dst, ld_src, ld_wgt, ld_x, ld_par = sem("ld_dst"), sem("ld_src"), sem("ld_wgt"), sem("ld_x"), sem("ld_par")
        diag_zeroed = sem("diag_zeroed")
        consts_ready = sem("consts_ready")
        meta_ready, meta_stored, meta_loaded = sem("meta_ready"), sem("meta_stored"), sem("meta_loaded")
        rel_ready, srcf_ready = sem("rel_ready"), sem("srcf_ready")
        edge_tr, edge_ev = sem("edge_tr"), sem("edge_ev")
        hist_ready, degmm_done, degs_ready = sem("hist_ready"), sem("degmm_done"), sem("degs_ready")
        deg_stored, deg_loaded = sem("deg_stored"), sem("deg_loaded")
        agg_zeroed = sem("agg_zeroed")
        flag_ready = sem("flag_ready")
        xc_ready, sq_ready = sem("xc_ready"), sem("sq_ready")
        chunk_ready, chunk_stored = sem("chunk_ready"), sem("chunk_stored")
        var_ready, sd_ready = sem("var_ready"), sem("sd_ready")
        dve_step, act_step, pool_step = sem("dve_step"), sem("act_step"), sem("pool_step")
        idx_staged, pool_turn = sem("idx_staged"), sem("pool_turn")
        gathered = [sem(f"gathered{s}") for s in range(SECTIONS)]
        cols_staged, act_turn = sem("cols_staged"), sem("act_turn")
        onehot_ready, summed, relued = sem("onehot_ready"), sem("summed"), sem("relued")
        agg_done, added = sem("agg_done"), sem("added")
        first_part, own_ready = sem("first_part"), sem("own_ready")
        id_staged, hot_ready, looked, row_ready = sem("id_staged"), sem("hot_ready"), sem("looked"), sem("row_ready")
        group_ready, quad_step = sem("group_ready"), sem("quad_step")
        ea_loaded = [sem(f"ea_loaded{s}") for s in range(SECTIONS)]
        ea_tr, ea_ev, ea_prod = sem("ea_tr"), sem("ea_ev"), sem("ea_prod")
        w0_tr, w0_ev = sem("w0_tr"), sem("w0_ev")
        mid_mm, mid_ev = sem("mid_mm"), sem("mid_ev")
        ht_mm, ht_ev = sem("ht_mm"), sem("ht_ev")
        z1_mm, z1_ev, z2_mm, z2_ev = sem("z1_mm"), sem("z1_ev"), sem("z2_mm"), sem("z2_ev")
        out_stored = sem("out_stored")
        gp_dst = sem("gp_dst")
        gp_ready = [sem(f"gp_ready{k}") for k in range(3)]
        gp_oh, gp_mm, gp_add = ([sem(f"{n}{k}") for k in range(3)] for n in ("gp_oh", "gp_mm", "gp_add"))
        gp_idx, gp_got, gp_msg = ([sem(f"{n}{k}") for k in range(2)] for n in ("gp_idx", "gp_got", "gp_msg"))
        gp_ea, gp_tr, gp_ev, gp_prod, gp_sum, gp_relu = (sem(n) for n in ("gp_ea", "gp_tr", "gp_ev", "gp_prod", "gp_sum", "gp_relu"))
        gp_step, layer_done = sem("gp_step"), sem("layer_done")
        iota_copied = sem("iota_copied")
        hist_step, sign_step = sem("hist_step"), sem("sign_step")
        block_ready, blocks_ready, over_ready, w0c_ready = (sem(n) for n in ("block_ready", "blocks_ready", "over_ready", "w0c_ready"))
        gp_row, gp_turn = sem("gp_row"), sem("gp_turn")
        gp_step2 = [sem(f"gp_shift{k}") for k in range(2)]

        def wait(eng, s, n):
            if not isinstance(n, int) or n > 0:
                eng.wait_ge(s, n)

        def linker(eng, s):
            count = [0]

            def link(ins):
                count[0] += 1
                ins.then_inc(s, 1)
                eng.wait_ge(s, count[0])
            return link

        def rounds(eng, body):
            body(0, True, False)
            with eng.Fori(1, ROUNDS - 1) as i:
                body(i, False, False)
            body(ROUNDS - 1, False, True)

        def rows_in(L, s, i):
            tiles = TILES - 1 if s == LAST else TILES
            return i * (16 * tiles) + 16 * (TILES + L * (TILES + (ROUNDS - 1) * tiles))

        def looks(L, i, step):
            return LOOKS * (L * ROUNDS + i) + step

        def look_of(i, s, first, last):
            if s == LAST:
                return None if last else (i + 1, 0)
            return (i, s + 1) if s + 1 < LOOKS and not first else None

        def one(i):
            return bass.ds(i, 1) if not isinstance(i, int) else slice(i, i + 1)

        def edge_rows(a):
            return a.rearrange("(r e) -> r e", e=RE)

        EDGE_T = [(a, k, min(GROUP4, TPR - k)) for a in range(3) for k in range(0, TPR, GROUP4)]
        HT_T = NC // GROUP4
        NMG = NC // MG
        PAIRS = -(-NC // (2 * GROUP4))

        def halves(n):
            return min(2, NC // GROUP4 - 2 * n)

        block = ctx.enter_context(nc.Block())

        @block.sync
        def _(sp):
            sp.dma_start(dst_e.bitcast(i32), edge_rows(dst)).then_inc(ld_dst, 16)
            sp.dma_start(src_e.bitcast(i32), edge_rows(src)).then_inc(ld_src, 16)
            sp.dma_start(xres[:, :, :], x.rearrange("(p c) d -> p c d", c=NC)).then_inc(ld_x, 16)
            sp.dma_start(wgt_e, edge_rows(edge_weight)).then_inc(ld_wgt, 16)
            sp.dma_start(w0_s[:, :], w0).then_inc(ld_par, 16)
            sp.dma_start(w1_s[:, :], w1).then_inc(ld_par, 16)
            for n, b in enumerate((b0, b2, be)):
                sp.dma_start(rows[:, n, :], b.partition_broadcast(NP)).then_inc(ld_par, 16)
            for h in range(2):
                sp.dma_start(b1_c[h * D:(h + 1) * D, :], b1.rearrange("(d o) -> d o", o=1)).then_inc(ld_par, 16)
            sp.wait_ge(diag_zeroed, 1)
            for h in range(2):
                sp.dma_start(w2_s[h * D:(h + 1) * D, h, :], w2).then_inc(ld_par, 16)
            for j in range(TILES - 1):
                sp.dma_start(we_s[j * ED:(j + 1) * ED, j, :], we).then_inc(ld_par, 16)
            sp.wait_ge(meta_ready, 1)
            sp.dma_start(meta_dram[0:NSEC].rearrange("(r s) -> r s", s=SECTIONS), meta_i[:, :]).then_inc(meta_stored, 16)
            sp.wait_ge(over_ready, 1)
            sp.dma_start(meta_dram[NSEC:].rearrange("(r o) -> r o", o=1), over[:, :].bitcast(i32)).then_inc(meta_stored, 16)
            sp.wait_ge(meta_stored, 32)
            sp.dma_start(meta_row[:, :], meta_dram.rearrange("(o k) -> o k", o=1)).then_inc(meta_loaded, 16)
            sp.wait_ge(flag_ready, 1)
            far = sp.value_load(flag_i[0:1, 0:1], min_val=0, max_val=1)

            def general_dst(k, after, n):
                sp.wait_ge(after, n)
                for s in range(SECTIONS):
                    sp.dma_start(left_i[:, :, s * TILES:(s + 1) * TILES].bitcast(i32),
                                 dst.rearrange("(r s p j) -> s p r j", s=SECTIONS, p=P, j=TILES)[s]).then_inc(gp_dst, 16)

            with sp.If(far > 0):
                general_dst(0, xc_ready, CH)
            sp.wait_ge(degs_ready, 1)
            sp.dma_start(deg_dram.rearrange("(g h l) -> h g l", g=HG, h=HP), degs[:, :, :]).then_inc(deg_stored, 16)
            sp.wait_ge(deg_stored, 16)
            sp.dma_start(deg[:, :], deg_dram[0:N].rearrange("(p c) -> p c", c=NC)).then_inc(deg_loaded, 16)

            def store_table(L):
                t = table_dram[L].rearrange("(p c) d -> p c d", c=NC)
                for c in range(CH):
                    sp.wait_ge(chunk_ready, L * CH + c + 1)
                    sp.dma_start(t[:, c * CHC:(c + 1) * CHC, :], tbl3[:, c * CHC:(c + 1) * CHC, :]).then_inc(chunk_stored, 16)

            store_table(0)
            with sp.If(far > 0):
                general_dst(1, agg_done, NSEC)
            store_table(1)

            def load_round(i, first, last):
                for s in range(SECTIONS):
                    if not first:
                        sp.wait_ge(ea_tr, 2 * (i * SECTIONS + s - SECTIONS + 1))
                    sp.dma_start(ea[:, s, :], ea_view[i, s]).then_inc(ea_loaded[s], 16)
            rounds(sp, load_round)
            with sp.If(far > 0):
                general_dst(2, agg_done, 2 * NSEC)
                sp.wait_ge(ea_prod, NSEC)
                with sp.Fori(0, ROUNDS) as i:
                    sp.wait_ge(gp_step, i + 1)
                    sp.dma_start(ea[:, :, :], edge_attr.rearrange("(r s p j) d -> r p s (j d)", s=SECTIONS, p=P, j=TILES)[i]).then_inc(gp_ea, 16)
            o = out.rearrange("(p c) d -> p c d", c=NC)
            for c in range(CH):
                sp.wait_ge(z2_ev, -(-(c + 1) * CHC // (2 * GROUP4)))
                sp.dma_start(o[:, c * CHC:(c + 1) * CHC, :], xres[:, c * CHC:(c + 1) * CHC, :]).then_inc(out_stored, 16)
            sp.wait_ge(out_stored, 16 * CH)

        @block.gpsimd
        def _(pool):
            link = linker(pool, pool_step)
            link(nc.gpsimd.memset(we_s[:, :, :], 0.0))
            nc.gpsimd.memset(w2_s[:, :, :], 0.0).then_inc(diag_zeroed, 1)
            link(nc.gpsimd.iota(iota_g[:, :], pattern=[[1, GEN]], base=0, channel_multiplier=0,
                                allow_small_or_imprecise_dtypes=True))
            link(nc.gpsimd.tensor_scalar(half_off[:, :], iota_g[:, 0:WINDOW + 1], -1.0, 0.5, ALU.mult, ALU.add))
            link(nc.gpsimd.iota(group_id[:, :], pattern=[[1, NG]], base=0, channel_multiplier=NG,
                                allow_small_or_imprecise_dtypes=True))
            link(nc.gpsimd.memset(ident[:, :], 0.0))
            nc.gpsimd.affine_select(out=ident[:, :], in_=ident[:, :], compare_op=ALU.not_equal, fill=1.0, base=0,
                                    pattern=[[-1, P]], channel_multiplier=1).then_inc(consts_ready, 1)
            pool.wait_ge(block_ready, 1)
            for n in range(LOG_W):
                size = float(WINDOW >> (n + 1))
                link(nc.gpsimd.tensor_scalar(bits[:, n, :], bl[:, :], size, None, ALU.is_ge))
                link(nc.gpsimd.tensor_scalar(bit_step[:, :], bits[:, n, :], size, None, ALU.mult))
                link(nc.gpsimd.tensor_tensor(bl[:, :], bl[:, :], bit_step[:, :], ALU.subtract))
            for s in range(SECTIONS):
                o = ohb_of(s)
                link(nc.gpsimd.memset(o[:, 0:1], 0.0))
                link(nc.gpsimd.tensor_scalar(o[:, 1:HI + 1], iota_g[0:ROUNDS, 0:HI], bh[:, s:s + 1], None, ALU.is_equal))
            pool.sem_inc(blocks_ready, 1)
            pool.wait_ge(ld_x, 16)
            half = D // 2
            link(nc.gpsimd.tensor_tensor(tbl3[:, :, 0:half], xres[:, :, 0:half], xres[:, :, half:D], ALU.add))
            while half > 1:
                half //= 2
                link(nc.gpsimd.tensor_tensor(tbl3[:, :, 0:half], tbl3[:, :, 0:half], tbl3[:, :, half:2 * half], ALU.add))
            link(nc.gpsimd.tensor_scalar(mean[:, :], tbl3[:, :, 0:1].rearrange("p c o -> p (c o)"), 1.0 / D, None, ALU.mult))
            for c in range(CH):
                cs = slice(c * CHC, (c + 1) * CHC)
                nc.gpsimd.tensor_tensor(xres[:, cs, :], xres[:, cs, :],
                                        mean[:, cs].unsqueeze(2).to_broadcast([NP, CHC, D]),
                                        ALU.subtract).then_inc(xc_ready, 1)
            for c in range(CH):
                cs = slice(c * CHC, (c + 1) * CHC)
                pool.wait_ge(xc_ready, c + 1)
                nc.gpsimd.tensor_tensor(hbuf[:, cs, :], xres[:, cs, :], xres[:, cs, :], ALU.mult).then_inc(sq_ready, 1)
            pool.wait_ge(edge_ev, len(EDGE_T))
            pool.wait_ge(over_ready, 1)
            pool.wait_ge(rel_ready, 2)
            nc.gpsimd.memset(agg[0:D, :], 0.0).then_inc(agg_zeroed, 1)
            pool.wait_ge(flag_ready, 1)
            far = pool.value_load(flag_i[0:1, 0:1], min_val=0, max_val=1)

            def gather(L, s, j, done):
                nc.gpsimd.indirect_dma_start(
                    out=g[:, s, j, :], out_offset=None, in_=table_dram[L][:, :],
                    in_offset=bass.IndirectOffsetOnAxis(ap=stage[:, s, j:j + 1], axis=0)).then_inc(done, 16)

            for L in range(2):
                if L == 1:
                    pool.wait_ge(ld_par, 16 * LOADS)
                    for c in range(CH):
                        cs = slice(c * CHC, (c + 1) * CHC)
                        pool.wait_ge(own_ready, c + 1)
                        nc.gpsimd.tensor_tensor(tbl3[:, cs, :], hbuf[:, cs, :],
                                                rows[:, 2, :].unsqueeze(1).to_broadcast([NP, CHC, D]),
                                                ALU.add).then_inc(chunk_ready, 1)
                pool.wait_ge(chunk_stored, 16 * CH * (L + 1))

                def gather_round(i, first, last):
                    for s in range(SECTIONS):
                        pool.wait_ge(idx_staged, (i + L * ROUNDS) * SECTIONS + s + 1)
                        pool.sem_inc(pool_turn, 1)
                        for j in range(TILES if first or s < LAST else TILES - 1):
                            gather(L, s, j, gathered[s])
                rounds(pool, gather_round)
                with pool.If(far > 0):
                    with pool.Fori(0, ROUNDS) as i:
                        pool.wait_ge(gp_idx[L], i + 1)
                        pool.sem_inc(pool_turn, 1)
                        for k in range(TPR):
                            gather(L, k // TILES, k % TILES, gp_got[L])

        @block.scalar
        def _(act):
            link = linker(act, act_step)
            act.wait_ge(consts_ready, 1)
            act.wait_ge(ld_src, 16)
            nc.scalar.copy(src_e, src_e.bitcast(i32)).then_inc(srcf_ready, 1)
            act.wait_ge(rel_ready, 2)
            link(nc.scalar.activation(hit_act, rel_b[:, :], ACT.Relu, bias=half_off[0:ROUNDS, WINDOW:WINDOW + 1],
                                      accum_out=over[:, :]))
            act.sem_inc(over_ready, 1)
            for s in range(SECTIONS):
                for w in range(W_ACT, WINDOW + 1):
                    n = s * (WINDOW + 1 - W_ACT) + w - W_ACT
                    wait(act, sign_step, n - 1)
                    nc.scalar.activation(hit_act[:, n % 2 * SEC_E:(n % 2 + 1) * SEC_E], rel_b[:, s * SEC_E:(s + 1) * SEC_E],
                                         ACT.Sign, bias=half_off[0:ROUNDS, w:w + 1],
                                         accum_out=signs[:, s, w - W_ACT:w - W_ACT + 1]).then_inc(sign_step, 1)
            for n, (a, k, m) in enumerate(EDGE_T):
                act.wait_ge(edge_tr, n + 1)
                to = (rel, idx, wgt)[a]
                nc.scalar.copy(to[:, :, k:k + m].rearrange("p r k -> p k r"),
                               ps[:, n % 4, 0:m * ROUNDS].rearrange("p (k r) -> p k r", r=ROUNDS)).then_inc(edge_ev, 1)
            act.wait_ge(w0_tr, 1)
            nc.scalar.copy(w0T[:, 0:D], ps[0:D, 7, 0:D]).then_inc(w0_ev, 1)

            def deviations(L):
                def root(c):
                    cs = slice(c * CHC, (c + 1) * CHC)
                    act.wait_ge(var_ready, L * (CH + 1) + c + 1)
                    nc.scalar.activation(rstd[:, cs], rstd[:, cs], ACT.Sqrt).then_inc(sd_ready, 1)

                for c in range(CH):
                    if L == 1:
                        act.wait_ge(xc_ready, CH + c + 1)
                        nc.scalar.activation(hbuf[:, c * CHC:(c + 1) * CHC, :], xres[:, c * CHC:(c + 1) * CHC, :],
                                             ACT.Square).then_inc(sq_ready, 1)
                    if c >= 1:
                        root(c - 1)
                root(CH - 1)
            deviations(0)
            act.wait_ge(flag_ready, 1)
            far = act.value_load(flag_i[0:1, 0:1], min_val=0, max_val=1)
            def stage_section(i, s):
                nc.scalar.copy(stage[:, s:s + 1, :], idx[:, one(i), s * TILES:(s + 1) * TILES]).then_inc(idx_staged, 1)
                nc.scalar.copy(cols[:, s:s + 1, :, :], relw[:, one(i), :, s * TILES:(s + 1) * TILES]).then_inc(cols_staged, 1)

            def stage_id(i):
                nc.scalar.copy(id_col[:, :], group[:, one(i)]).then_inc(id_staged, 1)

            act.wait_ge(edge_ev, len(EDGE_T))
            for s in range(SECTIONS):
                stage_section(0, s)
            act.wait_ge(var_ready, CH + 1)
            nc.scalar.activation(norm[:, :], norm[:, :], ACT.Sqrt).then_inc(sd_ready, 1)
            def stage_round(i, first, last):
                if not last:
                    for s in range(SECTIONS):
                        act.wait_ge(agg_done, i * SECTIONS + s + 1)
                        act.sem_inc(act_turn, 1)
                        stage_section(i + 1, s)
                        if s == 0:
                            stage_id(i + 1)
            def first_parts(L):
                act.wait_ge(chunk_stored, 16 * CH * (L + 1))
                for c in range(CH):
                    cs = slice(c * CHC, (c + 1) * CHC)
                    nc.scalar.copy(planes[:, 0, cs, :], tbl3[:, cs, :]).then_inc(first_part, 1)

            first_parts(0)
            act.wait_ge(group_ready, 1)
            rounds(act, stage_round)
            deviations(1)
            act.wait_ge(layer_done, 1)
            for s in range(SECTIONS):
                stage_section(0, s)
            aggc = agg[0:D, 0:N].rearrange("f (p c) -> f c p", c=NC)
            for n in range(HT_T):
                act.wait_ge(ht_mm, n + 1)
                nc.scalar.copy(aggc[:, n * GROUP4:(n + 1) * GROUP4, :],
                               ps[0:D, n % 4, 0:GROUP4 * NP].rearrange("f (c p) -> f c p", p=NP)).then_inc(ht_ev, 1)

            def evacuate(q, s, trd, evd, slot):
                t = tr_bank
                act.wait_ge(trd, 2 * q + 2)
                nc.scalar.copy(eaT[:, slot, 0, :], t[:, 0:P]).then_inc(evd, 1)
                nc.scalar.copy(eaT[0:ED, slot, 1, :], t[0:ED, P:2 * P]).then_inc(evd, 1)

            evacuate(0, 0, ea_tr, ea_ev, 0)
            first_parts(1)

            def act_round(i, first, last):
                for s in range(SECTIONS):
                    q = i * SECTIONS + s
                    act.wait_ge(summed, q + 1)
                    nc.scalar.activation(msg[:, s, :, :], msg[:, s, :, :], ACT.Relu).then_inc(relued, 1)
                    if not (last and s == SECTIONS - 1):
                        act.wait_ge(ea_prod, q + 1)
                        evacuate(q + 1, (s + 1) % SECTIONS, ea_tr, ea_ev, ((s + 1) % SECTIONS) % 2)
                    if not last:
                        stage_section(i + 1, s)
                        if s == 0:
                            stage_id(i + 1)
            rounds(act, act_round)
            with act.If(far > 0):
                with act.Fori(0, ROUNDS) as i:
                    for s in range(SECTIONS):
                        q = i * SECTIONS + s
                        evacuate(q, s, gp_tr, gp_ev, s % 2)
                        act.wait_ge(gp_sum, q + 1)
                        nc.scalar.activation(msg[:, s, :, :], msg[:, s, :, :], ACT.Relu).then_inc(gp_relu, 1)
            for n in range(PAIRS):
                act.wait_ge(z1_mm, n + 1)
                if n >= 1:
                    act.wait_ge(z2_mm, n)
                h = D * halves(n)
                nc.scalar.activation(r1[0:h, 0:GROUP4 * NP], ps[0:h, n % 2, 0:GROUP4 * NP], ACT.Relu,
                                     bias=b1_c[0:h, 0:1]).then_inc(z1_ev, 1)

        @block.vector
        def _(dve):
            link = linker(dve, dve_step)

            def combine(o, a, b, op=ALU.mult):
                return nc.vector.tensor_tensor(o, a, b, op)

            dve.wait_ge(ld_dst, 16)
            ds3 = dst_e.bitcast(i32).rearrange("r (s e) -> r s e", s=SECTIONS)
            rel3 = rel_e.rearrange("r (s e) -> r s e", s=SECTIONS)
            link(nc.vector.tensor_reduce(lo[:, :], ds3, AX.X, ALU.min))
            combine(rel3, ds3, lo[:, :].unsqueeze(2).to_broadcast([ROUNDS, SECTIONS, SEC_E]), ALU.subtract).then_inc(rel_ready, 1)
            nc.vector.tensor_copy(meta_i[:, :], lo[:, :]).then_inc(meta_ready, 1)
            dve.wait_ge(rel_ready, 1)
            nc.vector.tensor_copy(rel_b[:, :], rel_e).then_inc(rel_ready, 1)
            dve.wait_ge(meta_ready, 1)
            link(nc.vector.tensor_scalar(block_i[:, :], meta_i[:, :], LOG_W, None, ALU.arith_shift_right))
            link(nc.vector.tensor_copy(bh[:, :], block_i[:, :]))
            nc.vector.scalar_tensor_tensor(bl[:, :], bh[:, :], -float(WINDOW), lo[:, :], ALU.mult, ALU.add).then_inc(block_ready, 1)

            def variance(L, c):
                cs = slice(c * CHC, (c + 1) * CHC)
                dve.wait_ge(sq_ready, L * CH + c + 1)
                link(nc.vector.tensor_reduce(rstd[:, cs], hbuf[:, cs, :], AX.X, ALU.add))
                nc.vector.tensor_scalar(rstd[:, cs], rstd[:, cs], 1.0 / D, EPS, ALU.mult, ALU.add).then_inc(var_ready, 1)

            link(nc.vector.memset(hist[:, :, :], 0.0))
            dve.wait_ge(rel_ready, 2)
            for s in range(SECTIONS):
                for w in range(W_ACT):
                    n = s * W_ACT + w
                    wait(dve, hist_step, n - 1)
                    nc.vector.tensor_scalar(hit[:, n % 2, :], rel_b[:, s * SEC_E:(s + 1) * SEC_E], float(w), 0.0,
                                            ALU.is_equal, ALU.add,
                                            accum_out=hist[:, s, PAD + w:PAD + w + 1]).then_inc(hist_step, 1)
            dve.wait_ge(sign_step, SECTIONS * (WINDOW + 1 - W_ACT))
            dve.wait_ge(hist_step, SECTIONS * W_ACT)
            n = WINDOW - W_ACT
            link(combine(signs[:, :, 0:n], signs[:, :, 0:n], signs[:, :, 1:n + 1], ALU.subtract))
            link(nc.vector.tensor_scalar(hist[:, :, PAD + W_ACT:PAD + WINDOW], signs[:, :, 0:n], 0.5, None, ALU.mult))
            dve.wait_ge(blocks_ready, 1)
            for n in range(LOG_W):
                sh = WINDOW >> (n + 1)
                h0 = hist[:, :, PAD:PAD + 2 * WINDOW]
                link(combine(histd[:, :, :], hist[:, :, PAD - sh:PAD - sh + 2 * WINDOW], h0, ALU.subtract))
                link(combine(histd[:, :, :], histd[:, :, :],
                         bits[:, n, :].unsqueeze(2).to_broadcast([ROUNDS, SECTIONS, 2 * WINDOW])))
                link(combine(h0, h0, histd[:, :, :], ALU.add))
            dve.sem_inc(hist_ready, 1)
            dve.wait_ge(meta_loaded, 16)
            link(nc.vector.tensor_reduce(flag_f[:, :], meta_row[:, NSEC:], AX.X, ALU.max))
            link(nc.vector.tensor_scalar(flag_f[:, :], flag_f[:, :], 0.0, None, ALU.is_gt))
            nc.vector.tensor_copy(flag_i[:, :], flag_f[:, :]).then_inc(flag_ready, 1)
            for c in range(EARLY):
                variance(0, c)
            dve.wait_ge(degmm_done, 1)
            link(nc.vector.tensor_copy(degs[:, :, :].rearrange("h g l -> h (g l)"), ps[0:HP, 6, 0:HG * WINDOW]))
            far = dve.value_load(flag_i[0:1, 0:1], min_val=0, max_val=1)

            def far_edges(k):
                dve.wait_ge(gp_dst, 16 * SECTIONS * (k + 1))
                nc.vector.tensor_copy(left, left_i.bitcast(i32)).then_inc(gp_ready[k], 1)
                dve.wait_ge(gp_ready[k], 1)
                nc.vector.tensor_scalar(left, left, FAR, None, ALU.subtract).then_inc(gp_ready[k], 1)
                nc.vector.tensor_scalar(left_i, rel[:, :, :], float(WINDOW), None, ALU.is_ge).then_inc(gp_ready[k], 1)
                dve.wait_ge(gp_ready[k], 3)
                combine(left, left, left_i).then_inc(gp_ready[k], 1)
                dve.wait_ge(gp_ready[k], 4)
                nc.vector.tensor_scalar(left, left, FAR, None, ALU.add).then_inc(gp_ready[k], 1)
                dve.wait_ge(gp_ready[k], 5)

            with dve.If(far > 0):
                far_edges(0)
                nc.vector.tensor_copy(left_i.bitcast(i32), left).then_inc(gp_ready[0], 1)
                dve.wait_ge(gp_ready[0], 6)
                nc.vector.tensor_scalar(left_i.bitcast(i32), left_i.bitcast(i32), LOG_W, None,
                                        ALU.arith_shift_right).then_inc(gp_ready[0], 1)
                dve.wait_ge(gp_ready[0], 7)
                nc.vector.tensor_copy(left_i, left_i.bitcast(i32)).then_inc(gp_ready[0], 1)
                dve.wait_ge(gp_ready[0], 8)
                nc.vector.scalar_tensor_tensor(left, left_i, -float(WINDOW), left, ALU.mult, ALU.add).then_inc(gp_ready[0], 1)
                dve.wait_ge(gp_ready[0], 9)
                with dve.Fori(0, ROUNDS) as i:
                    nc.vector.tensor_copy(shift[:, :], left_i[:, bass.ds(i, 1), :].rearrange("p o k -> p (o k)")).then_inc(gp_row, 1)
                    nc.vector.tensor_copy(shift_lo[:, :], left[:, bass.ds(i, 1), :].rearrange("p o k -> p (o k)")).then_inc(gp_row, 1)
                    dve.wait_ge(gp_row, 2 * (i + 1))
                    for k in range(TPR):
                        n = i * TPR + k
                        nc.vector.tensor_scalar(wide[:, 0:HI], iota_g[:, 0:HI], shift[:, k:k + 1], None,
                                                ALU.is_equal).then_inc(gp_oh[0], 1)
                        nc.vector.tensor_scalar(oh[:, 0, 0, :], iota_g[:, 0:WINDOW], shift_lo[:, k:k + 1], None,
                                                ALU.is_equal).then_inc(gp_oh[0], 1)
                        dve.wait_ge(gp_mm[0], n + 1)
                        combine(degs[:, :, :].rearrange("h g l -> h (g l)"), degs[:, :, :].rearrange("h g l -> h (g l)"),
                            ps[0:HP, 4, 0:HG * WINDOW], ALU.add).then_inc(gp_add[0], 1)
                        dve.wait_ge(gp_add[0], n + 1)
            dve.sem_inc(degs_ready, 1)
            for c in range(EARLY, CH):
                variance(0, c)
            dve.wait_ge(sd_ready, CH)
            link(nc.vector.reciprocal(rstd[:, :], rstd[:, :]))
            dve.wait_ge(deg_loaded, 16)
            nc.vector.tensor_scalar(norm[:, :], deg[:, :], 1.0, None, ALU.max).then_inc(var_ready, 1)
            dve.wait_ge(sd_ready, CH + 1)
            link(nc.vector.reciprocal(norm[:, :], norm[:, :]))
            link(nc.vector.tensor_scalar(deg[:, :], deg[:, :], 0.0, None, ALU.is_gt))
            link(combine(norm[:, :], norm[:, :], deg[:, :]))
            link(combine(rstd[:, :], rstd[:, :], norm[:, :]))

            def normed_rows(c, to):
                cs = slice(c * CHC, (c + 1) * CHC)
                return nc.vector.scalar_tensor_tensor(to[:, cs, :], xres[:, cs, :], 0.0,
                                                      rstd[:, cs].unsqueeze(2).to_broadcast([NP, CHC, D]),
                                                      ALU.max, ALU.mult)
            for c in range(CH):
                normed_rows(c, tbl3).then_inc(chunk_ready, 1)
            dve.wait_ge(ld_par, 16 * LOADS)
            link(nc.vector.tensor_reduce(b0_mean[:, :], rows[:, 0, :], AX.X, ALU.add))
            link(nc.vector.tensor_scalar(b0_mean[:, :], b0_mean[:, :], 1.0 / D, None, ALU.mult))
            link(nc.vector.tensor_scalar(rows[:, 0, :], rows[:, 0, :], b0_mean[:, 0:1], None, ALU.subtract))
            link(nc.vector.tensor_scalar(mean[:, :], mean[:, :], b0_mean[:, 0:1], None, ALU.add))
            dve.wait_ge(w0_ev, 1)
            link(nc.vector.tensor_reduce(w0T[:, D:D + 1], w0T[:, 0:D], AX.X, ALU.add))
            link(nc.vector.tensor_scalar(w0T[:, D:D + 1], w0T[:, D:D + 1], 1.0 / D, None, ALU.mult))
            nc.vector.tensor_scalar(w0T[:, 0:D], w0T[:, 0:D], w0T[:, D:D + 1], None, ALU.subtract).then_inc(w0c_ready, 1)
            dve.wait_ge(edge_ev, len(EDGE_T))
            nodes = idx[:, :, TPR - 1:].rearrange("p r o -> p (r o)")
            link(nc.vector.tensor_copy(shifted.bitcast(i32), nodes))
            link(nc.vector.tensor_scalar(shifted.bitcast(i32), shifted.bitcast(i32), LOG_Q, None, ALU.arith_shift_right))
            link(nc.vector.tensor_copy(group[:, :], shifted.bitcast(i32)))
            link(nc.vector.scalar_tensor_tensor(offset, group[:, :], -float(QUAD), nodes, ALU.mult, ALU.add))
            combine(place[:, :, :], offset.unsqueeze(2).to_broadcast([P, ROUNDS, QUAD]),
                iota_g[:, 0:QUAD].unsqueeze(1).to_broadcast([P, ROUNDS, QUAD]), ALU.is_equal).then_inc(group_ready, 1)
            dve.wait_ge(group_ready, 1)
            nc.vector.tensor_copy(iota_p, iota_g[:, 0:WINDOW]).then_inc(iota_copied, 1)
            dve.wait_ge(iota_copied, 1)
            dve.wait_ge(agg_zeroed, 1)

            def layer(L):
                if L == 0:
                    dve.wait_ge(chunk_ready, CH)
                    link(combine(xres[:, :, :], xres[:, :, :], rows[:, 0, :].unsqueeze(1).to_broadcast([NP, NC, D]), ALU.add))
                else:
                    dve.wait_ge(own_ready, CH)
                    link(combine(xres[:, :, :], xres[:, :, :], mean[:, :].unsqueeze(2).to_broadcast([NP, NC, D]), ALU.add))
                    link(combine(xres[:, :, :], xres[:, :, :], rows[:, 1, :].unsqueeze(1).to_broadcast([NP, NC, D]), ALU.add))
                    dve.wait_ge(ht_ev, HT_T)

                def split(c):
                    cs = slice(c * CHC, (c + 1) * CHC)
                    r = msg[0:NP, :, :, :].rearrange("p s j d -> p (s j) d")[:, 0:CHC, :]
                    dve.wait_ge(first_part, L * CH + c + 1)
                    link(combine(r, tbl3[:, cs, :], planes[:, 0, cs, :], ALU.subtract))
                    link(nc.vector.tensor_copy(planes[:, 1, cs, :], r))
                    link(combine(planes[:, 2, cs, :], r, planes[:, 1, cs, :], ALU.subtract))

                dve.wait_ge(chunk_stored, 16 * CH * (L + 1))

                def found_rows(i):
                    base = 3 * L * ROUNDS
                    for h in range(2):
                        nc.vector.tensor_reduce(quad[:, h * QUAD // 2:(h + 1) * QUAD // 2, :],
                                                rows_p[h].rearrange("p (t o d) -> p o d t", t=PARTS, d=D),
                                                AX.X, ALU.add).then_inc(quad_step, 1)
                    dve.wait_ge(quad_step, 3 * i + base + 2)
                    combine(quad[:, :, :], quad[:, :, :], place[:, one(i), :].rearrange("p r o -> p (r o)").unsqueeze(2)
                        .to_broadcast([P, QUAD, D])).then_inc(quad_step, 1)
                    dve.wait_ge(quad_step, 3 * i + base + 3)
                    nc.vector.tensor_reduce(g[:, LAST, TILES - 1, :], quad[:, :, :].rearrange("p o d -> p d o"),
                                            AX.X, ALU.add).then_inc(row_ready, 1)

                def dve_round(i, first, last):
                    if first:
                        dve.sem_inc(hot_ready, LOOKS)
                        dve.sem_inc(quad_step, 3)
                    for s in range(SECTIONS):
                        q = i * SECTIONS + s
                        Q = q + L * NSEC
                        base = dve.value_load(meta_row[0:1, one(q)],
                                              min_val=0, max_val=N - 1)
                        dve.wait_ge(cols_staged, Q + 1)
                        for j in range(TILES):
                            lastoh = nc.vector.tensor_scalar(oh[:, s, j, :], iota_p, cols[:, s, 0, j:j + 1],
                                                             cols[:, s, 1, j:j + 1] if L == 0 else None,
                                                             ALU.is_equal, *([ALU.mult] if L == 0 else []))
                        lastoh.then_inc(onehot_ready, 1)
                        if not first and s == LAST:
                            dve.wait_ge(looked, LOOKS + looks(L, i + 1, 0))
                            found_rows(i)
                        if L == 1:
                            dve.wait_ge(gathered[s], rows_in(1, s, i))
                            if not first and s == LAST:
                                dve.wait_ge(row_ready, ROUNDS - 1 + i)
                            dve.wait_ge(ea_prod, q + 1)
                            combine(msg[:, s, :, :], mbank(s).rearrange("p (j d) -> p j d", d=D), g[:, s, :, :],
                                ALU.add).then_inc(summed, 1)
                        look = look_of(i, s, first, last)
                        if look:
                            n, (g0, g1) = looks(L, *look), STEPS[look[1]:look[1] + 2]
                            dve.wait_ge(looked, n + 1)
                            combine(hot[:, g0:g1, :], ids_p.unsqueeze(1).to_broadcast([NP, g1 - g0, P]),
                                group_id[:, g0:g1].unsqueeze(2).to_broadcast([NP, g1 - g0, P]),
                                ALU.is_equal).then_inc(hot_ready, 1)
                        dve.wait_ge(agg_done, Q + 1)
                        wait(dve, added, Q)
                        a = agg[0:D, bass.ds(base, WINDOW)]
                        combine(a, a, win(s), ALU.add).then_inc(added, 1)
                        if first and s < LAST:
                            for c in range(s * CH // LAST, (s + 1) * CH // LAST):
                                split(c)
                rounds(dve, dve_round)
                dve.wait_ge(added, NSEC * (L + 1))
                with dve.If(far > 0):
                    far_edges(L + 1)
                    with dve.Fori(0, ROUNDS) as i:
                        nc.vector.tensor_copy(shift[:, :], left[:, bass.ds(i, 1), :].rearrange("p o k -> p (o k)")).then_inc(gp_step2[L], 1)
                        nc.vector.tensor_copy(stage[:, :, :].rearrange("p s j -> p (s j)"),
                                              idx[:, bass.ds(i, 1), :].rearrange("p o k -> p (o k)")).then_inc(gp_idx[L], 1)
                        dve.wait_ge(gp_got[L], (i + 1) * 16 * TPR)
                        if L == 0:
                            combine(msg[:, :, :, :].rearrange("p s j d -> p (s j) d"), g[:, :, :, :].rearrange("p s j d -> p (s j) d"),
                                wgt[:, bass.ds(i, 1), :].rearrange("p o k -> p (o k)").unsqueeze(2).to_broadcast([P, TPR, D])
                                ).then_inc(gp_msg[0], 1)
                        else:
                            for s in range(SECTIONS):
                                dve.wait_ge(gp_prod, i * SECTIONS + s + 1)
                                combine(msg[:, s, :, :], mbank(s).rearrange("p (j d) -> p j d", d=D), g[:, s, :, :],
                                    ALU.add).then_inc(gp_sum, 1)
                        with dve.Fori(0, NGEN) as v:
                            for k in range(TPR):
                                n = (i * NGEN + v) * TPR + k
                                if k == 0:
                                    dve.wait_ge(gp_step2[L], i * (NGEN + 1) + v + 1)
                                nc.vector.tensor_scalar(wide[:, :], iota_g[:, :], shift[:, k:k + 1], None,
                                                        ALU.is_equal).then_inc(gp_oh[L + 1], 1)
                                dve.wait_ge(gp_mm[L + 1], n + 1)
                            nc.vector.tensor_scalar(shift[:, :], shift[:, :], float(GEN), None, ALU.subtract).then_inc(gp_step2[L], 1)
                            a = agg[0:D, bass.ds(v * GEN, GEN)]
                            combine(a, a, ps[0:D, 7, 0:GEN], ALU.add).then_inc(gp_add[L + 1], 1)
                            dve.wait_ge(gp_add[L + 1], i * NGEN + v + 1)
                dve.sem_inc(layer_done, 1)

            layer(0)
            def finish(c):
                cs = slice(c * CHC, (c + 1) * CHC)
                dve.wait_ge(sd_ready, CH + 1 + c + 1)
                link(nc.vector.reciprocal(rstd[:, cs], rstd[:, cs]))
                normed_rows(c, hbuf).then_inc(own_ready, 1)

            for n in range(NMG):
                cs = slice(n * MG, (n + 1) * MG)
                p = ps[0:NP, n % 4, 0:MG * (D + 1)].rearrange("p (c d) -> p c d", d=D + 1)
                c = (n + 1) * MG // CHC - 1
                dve.wait_ge(mid_mm, n + 1)
                combine(scratch[:, n % 2, :, :], p, norm[:, cs].unsqueeze(2).to_broadcast([NP, MG, D + 1])).then_inc(mid_ev, 1)
                dve.wait_ge(mid_ev, n + 1)
                combine(mean[:, cs], mean[:, cs], scratch[:, n % 2, :, D:D + 1].rearrange("p c o -> p (c o)"), ALU.add)
                last = combine(xres[:, cs, :], xres[:, cs, :], scratch[:, n % 2, :, 0:D], ALU.add)
                if (n + 1) * MG % CHC == 0:
                    last.then_inc(xc_ready, 1)
                    if c >= 1:
                        variance(1, c - 1)
                    if c >= 2:
                        finish(c - 2)
            finish(CH - 2)
            variance(1, CH - 1)
            finish(CH - 1)
            layer(1)
            for n in range(PAIRS):
                h = halves(n)
                cs = slice(2 * n * GROUP4, (2 * n + h) * GROUP4)
                a = xres[:, cs, :].rearrange("p (h c) d -> p h c d", h=h)
                dve.wait_ge(z2_mm, n + 1)
                combine(a, a, ps[0:NP, 2 + n % 2, 0:GROUP4 * h * D].rearrange("p (c h d) -> p h c d", h=h, d=D),
                    ALU.add).then_inc(z2_ev, 1)

        @block.tensor
        def _(pe):
            pe.wait_ge(consts_ready, 1)
            pe.wait_ge(ld_par, 16 * LOADS)
            nc.tensor.transpose(ps[0:D, 7, 0:D], w0_s[:, :], ident[0:D, 0:D]).then_inc(w0_tr, 1)
            for n, (a, k, m) in enumerate(EDGE_T):
                if k == 0:
                    if a == 0:
                        pe.wait_ge(rel_ready, 2)
                    elif a == 1:
                        pe.wait_ge(srcf_ready, 1)
                    else:
                        pe.wait_ge(ld_wgt, 16)
                if n >= 4:
                    pe.wait_ge(edge_ev, n - 3)
                arr = (rel_e, src_e, wgt_e)[a].rearrange("r (s p j) -> r s j p", s=SECTIONS, p=P)
                for t in range(m):
                    last = nc.tensor.transpose(ps[:, n % 4, t * ROUNDS:(t + 1) * ROUNDS],
                                               arr[:, (k + t) // TILES, (k + t) % TILES, :], ident[0:ROUNDS, 0:ROUNDS])
                last.then_inc(edge_tr, 1)
            pe.wait_ge(blocks_ready, 1)
            pe.wait_ge(hist_ready, 1)
            for gp in range(HG):
                steps = [(s, half) for s in range(SECTIONS) for half in range(2)]
                for n, (s, half) in enumerate(steps):
                    o = ohb_of(s)
                    last = nc.tensor.matmul(ps[0:HP, 6, gp * WINDOW:(gp + 1) * WINDOW],
                                            o[:, 1 - half + gp * HP:1 - half + (gp + 1) * HP],
                                            hist[:, s, PAD + half * WINDOW:PAD + (half + 1) * WINDOW],
                                            start=(n == 0), stop=(n == len(steps) - 1))
            last.then_inc(degmm_done, 1)
            pe.wait_ge(flag_ready, 1)
            far = pe.value_load(flag_i[0:1, 0:1], min_val=0, max_val=1)
            with pe.If(far > 0):
                with pe.Fori(0, ROUNDS) as i:
                    for k in range(TPR):
                        pe.wait_ge(gp_oh[0], 2 * (i * TPR + k + 1))
                        for gp in range(HG):
                            last = nc.tensor.matmul(ps[0:HP, 4, gp * WINDOW:(gp + 1) * WINDOW],
                                                    wide[:, gp * HP:(gp + 1) * HP], oh[:, 0, 0, :], start=True, stop=True)
                        last.then_inc(gp_mm[0], 1)

            def transposes(s, done):
                t = tr_bank
                cut = (TILES - 1) * ED
                nc.tensor.transpose(t[:, 0:P], ea[:, s, 0:cut], ident[:, :]).then_inc(done, 1)
                nc.tensor.transpose(t[0:ED, P:2 * P], ea[:, s, cut:cut + ED], ident[:, :]).then_inc(done, 1)

            def products(s, done):
                nc.tensor.matmul(mbank(s)[:, 0:(TILES - 1) * D], eaT[:, s % 2, 0, :],
                                 we_s[:, :, :].rearrange("p j d -> p (j d)"), start=True, stop=True)
                last = nc.tensor.matmul(mbank(s)[:, (TILES - 1) * D:], eaT[0:ED, s % 2, 1, :], we_s[0:ED, 0, :],
                                        start=True, stop=True)
                last.then_inc(done, 1)

            def window_sums(rows_of, s):
                for j in range(TILES):
                    last = nc.tensor.matmul(win(s), rows_of[:, s, j, :], oh[:, s, j, :], start=(j == 0), stop=(j == TILES - 1))
                last.then_inc(agg_done, 1)

            def turn_attributes(s, i):
                pe.wait_ge(ea_loaded[s], 16 * (i + 1))
                transposes(s, ea_tr)

            def use_attributes(q, s):
                pe.wait_ge(ea_ev, 2 * (q + 1))
                products(s, ea_prod)

            def look_up(L, i, step):
                pe.wait_ge(hot_ready, looks(L, i, step) + 1)
                for c in range(STEPS[step], STEPS[step + 1]):
                    for h in range(2):
                        k = c * QUAD + h * QUAD // 2
                        last = nc.tensor.matmul(rows_p[h], hot[:, c, :], planes[:, 0:PARTS, k:k + QUAD // 2, :],
                                                start=(c == 0), stop=(c == NG - 1))
                last.then_inc(looked, 1)

            pe.sem_inc(looked, LOOKS)
            for L in range(2):
                if L == 1:
                    turn_attributes(0, 0)
                    use_attributes(0, 0)

                def pe_round(i, first, last):
                    if first:
                        pe.sem_inc(looked, LOOKS)
                    for s in range(SECTIONS):
                        q = i * SECTIONS + s
                        ahead = L == 1 and not (last and s == LAST)
                        if ahead:
                            turn_attributes((s + 1) % SECTIONS, i + (1 if s == LAST else 0))
                        pe.wait_ge(onehot_ready, q + L * NSEC + 1)
                        if not last and s == LAST - 1:
                            pe.wait_ge(id_staged, L * (ROUNDS - 1) + i + 1)
                            nc.tensor.matmul(ids_p, id_col[:, 0:1].to_broadcast([P, NP]), ident[:, :], start=True, stop=True)
                        if L == 0:
                            pe.wait_ge(gathered[s], rows_in(0, s, i))
                            if not first and s == LAST:
                                pe.wait_ge(row_ready, i)
                            window_sums(g, s)
                        else:
                            pe.wait_ge(relued, q + 1)
                            window_sums(msg, s)
                        if ahead:
                            use_attributes(q + 1, (s + 1) % SECTIONS)
                        look = look_of(i, s, first, last)
                        if look:
                            look_up(L, *look)
                rounds(pe, pe_round)
                with pe.If(far > 0):
                    with pe.Fori(0, ROUNDS) as i:
                        if L == 0:
                            pe.wait_ge(gp_msg[0], i + 1)
                        else:
                            pe.sem_inc(gp_step, 1)
                            pe.wait_ge(gp_ea, 16 * (i + 1))
                            for s in range(SECTIONS):
                                transposes(s, gp_tr)
                                pe.wait_ge(gp_ev, 2 * (i * SECTIONS + s + 1))
                                products(s, gp_prod)
                                pe.wait_ge(gp_relu, i * SECTIONS + s + 1)
                        pe.sem_inc(gp_turn, 1)
                        with pe.Fori(0, NGEN) as v:
                            for k in range(TPR):
                                pe.wait_ge(gp_oh[L + 1], (i * NGEN + v) * TPR + k + 1)
                                nc.tensor.matmul(ps[0:D, 7, 0:GEN], msg[:, k // TILES, k % TILES, :], wide[:, :],
                                                 start=(k == 0), stop=(k == TPR - 1)).then_inc(gp_mm[L + 1], 1)
                pe.wait_ge(layer_done, L + 1)
                aggc = agg[0:D, 0:N].rearrange("f (p c) -> f c p", c=NC)
                if L == 0:
                    pe.wait_ge(w0c_ready, 1)
                    for n in range(NMG):
                        if n >= 4:
                            pe.wait_ge(mid_ev, n - 3)
                        for c in range(MG):
                            last = nc.tensor.matmul(ps[0:NP, n % 4, c * (D + 1):(c + 1) * (D + 1)],
                                                    aggc[:, n * MG + c, :], w0T[:, :], start=True, stop=True)
                        last.then_inc(mid_mm, 1)
                    pe.wait_ge(own_ready, CH)
                    for n in range(HT_T):
                        if n >= 4:
                            pe.wait_ge(ht_ev, n - 3)
                        for c in range(GROUP4):
                            last = nc.tensor.transpose(ps[0:D, n % 4, c * NP:(c + 1) * NP], hbuf[:, n * GROUP4 + c, :],
                                                       ident[0:NP, 0:NP])
                        last.then_inc(ht_mm, 1)
                    pe.wait_ge(ht_ev, HT_T)
                else:
                    def first_product(n):
                        if n >= 2:
                            pe.wait_ge(z1_ev, n - 1)
                        for h in range(halves(n)):
                            k = (2 * n + h) * GROUP4
                            last = nc.tensor.matmul(ps[h * D:(h + 1) * D, n % 2, 0:GROUP4 * NP], w1_s[:, :],
                                                    aggc[:, k:k + GROUP4, :], start=True, stop=True)
                        last.then_inc(z1_mm, 1)
                    first_product(0)
                    for n in range(PAIRS):
                        if n + 1 < PAIRS:
                            first_product(n + 1)
                        pe.wait_ge(z1_ev, n + 1)
                        if n >= 2:
                            pe.wait_ge(z2_ev, n - 1)
                        h = halves(n) * D
                        for c in range(GROUP4):
                            last = nc.tensor.matmul(ps[0:NP, 2 + n % 2, c * h:(c + 1) * h], r1[0:h, c * NP:(c + 1) * NP],
                                                    w2_s[0:h, :, :].rearrange("p h d -> p (h d)")[:, 0:h],
                                                    start=True, stop=True)
                        last.then_inc(z2_mm, 1)


_INS = ['x', 'src', 'dst', 'edge_attr_32', 'edge_weight', 'L0_gnn_weight', 'L0_gnn_b', 'L1_gnn_We', 'L1_gnn_be',
        'L1_gnn_W1', 'L1_gnn_b1', 'L1_gnn_W2', 'L1_gnn_b2']


def kernel(**inputs):
    import numpy as _np
    import concourse.bacc as _bacc
    from concourse import mybir as _mybir
    from concourse.bass_utils import run_bass_kernel_spmd as _run

    nc = _bacc.Bacc("TRN2", target_bir_lowering=False, num_devices=1)
    arrays, args = {}, []
    for name in _INS:
        a = _np.ascontiguousarray(inputs[name])
        arrays[f"in_{name}_dram"] = a
        args.append(nc.dram_tensor(f"in_{name}_dram", a.shape, _mybir.dt.from_np(a.dtype), kind="ExternalInput").ap())
    out = nc.dram_tensor("out_0_dram", inputs['x'].shape, _mybir.dt.float32, kind="ExternalOutput").ap()
    gnn_preln_two_layers(nc, *args, out)
    r = _run(nc, [arrays], core_ids=[0])
    return r.results[0]["out_0_dram"]
```
